# Optimizing a Trainium2 kernel written in Bass

```python
import numpy as np
import jax
import jax.numpy as jnp

def _softmax(x, axis=-1):
    return jax.nn.softmax(x, axis=axis)

def _gelu(x):
    return jax.nn.gelu(x, approximate=True)

def _silu(x):
    return jax.nn.silu(x)

def _sigmoid(x):
    return jax.nn.sigmoid(x)

def _layernorm(x, axis=-1, eps=1e-05):
    m = jnp.mean(x, axis=axis, keepdims=True)
    v = jnp.var(x, axis=axis, keepdims=True)
    return (x - m) / jnp.sqrt(v + eps)

def _scatter_add(tgt, idx, src, axis=0):
    return tgt.at[idx].add(src)

def _segment_sum(src, seg, n):
    return jax.ops.segment_sum(src, seg, n)
kernel_name = 'mk_dlrm_tower_d1_rec_r8_8b0d45'

def setup_inputs(seed: int=0):
    np.random.seed(seed)
    _w = jnp.asarray

    def _rec_inputs():
        import jax
        import jax.numpy as jnp
        _tk = jax.random.key(seed)
        dense_ctx = jax.random.normal(jax.random.fold_in(_tk, 190), (2048, 16), jnp.float32)
        ids = jnp.stack([jax.random.randint(jax.random.fold_in(_tk, 200 + f), (2048,), 0, v, jnp.int32) for f, v in enumerate([12500, 125000, 1000, 1250, 125000, 1000, 125000, 1000, 1000, 1250, 1250, 12500, 1000, 12500, 1000, 1250, 1250, 1250, 1250, 1000, 1000, 12500, 1000, 1000, 1250, 12500, 12500, 1250, 1000, 1000, 1000, 12500, 1000, 1250, 1250, 1000, 1250, 1000, 1000])], axis=1)
        tbl_0 = 0.05 * jax.random.normal(jax.random.fold_in(_tk, 500 + 0), (12500, 64), jnp.float32)
        tbl_1 = 0.05 * jax.random.normal(jax.random.fold_in(_tk, 500 + 1), (125000, 64), jnp.float32)
        tbl_2 = 0.05 * jax.random.normal(jax.random.fold_in(_tk, 500 + 2), (1000, 64), jnp.float32)
        tbl_3 = 0.05 * jax.random.normal(jax.random.fold_in(_tk, 500 + 3), (1250, 64), jnp.float32)
        tbl_4 = 0.05 * jax.random.normal(jax.random.fold_in(_tk, 500 + 4), (125000, 64), jnp.float32)
        tbl_5 = 0.05 * jax.random.normal(jax.random.fold_in(_tk, 500 + 5), (1000, 64), jnp.float32)
        tbl_6 = 0.05 * jax.random.normal(jax.random.fold_in(_tk, 500 + 6), (125000, 64), jnp.float32)
        tbl_7 = 0.05 * jax.random.normal(jax.random.fold_in(_tk, 500 + 7), (1000, 64), jnp.float32)
        tbl_8 = 0.05 * jax.random.normal(jax.random.fold_in(_tk, 500 + 8), (1000, 64), jnp.float32)
        tbl_9 = 0.05 * jax.random.normal(jax.random.fold_in(_tk, 500 + 9), (1250, 64), jnp.float32)
        tbl_10 = 0.05 * jax.random.normal(jax.random.fold_in(_tk, 500 + 10), (1250, 64), jnp.float32)
        tbl_11 = 0.05 * jax.random.normal(jax.random.fold_in(_tk, 500 + 11), (12500, 64), jnp.float32)
        tbl_12 = 0.05 * jax.random.normal(jax.random.fold_in(_tk, 500 + 12), (1000, 64), jnp.float32)
        tbl_13 = 0.05 * jax.random.normal(jax.random.fold_in(_tk, 500 + 13), (12500, 64), jnp.float32)
        tbl_14 = 0.05 * jax.random.normal(jax.random.fold_in(_tk, 500 + 14), (1000, 64), jnp.float32)
        tbl_15 = 0.05 * jax.random.normal(jax.random.fold_in(_tk, 500 + 15), (1250, 64), jnp.float32)
        tbl_16 = 0.05 * jax.random.normal(jax.random.fold_in(_tk, 500 + 16), (1250, 64), jnp.float32)
        tbl_17 = 0.05 * jax.random.normal(jax.random.fold_in(_tk, 500 + 17), (1250, 64), jnp.float32)
        tbl_18 = 0.05 * jax.random.normal(jax.random.fold_in(_tk, 500 + 18), (1250, 64), jnp.float32)
        tbl_19 = 0.05 * jax.random.normal(jax.random.fold_in(_tk, 500 + 19), (1000, 64), jnp.float32)
        tbl_20 = 0.05 * jax.random.normal(jax.random.fold_in(_tk, 500 + 20), (1000, 64), jnp.float32)
        tbl_21 = 0.05 * jax.random.normal(jax.random.fold_in(_tk, 500 + 21), (12500, 64), jnp.float32)
        tbl_22 = 0.05 * jax.random.normal(jax.random.fold_in(_tk, 500 + 22), (1000, 64), jnp.float32)
        tbl_23 = 0.05 * jax.random.normal(jax.random.fold_in(_tk, 500 + 23), (1000, 64), jnp.float32)
        tbl_24 = 0.05 * jax.random.normal(jax.random.fold_in(_tk, 500 + 24), (1250, 64), jnp.float32)
        tbl_25 = 0.05 * jax.random.normal(jax.random.fold_in(_tk, 500 + 25), (12500, 64), jnp.float32)
        tbl_26 = 0.05 * jax.random.normal(jax.random.fold_in(_tk, 500 + 26), (12500, 64), jnp.float32)
        tbl_27 = 0.05 * jax.random.normal(jax.random.fold_in(_tk, 500 + 27), (1250, 64), jnp.float32)
        tbl_28 = 0.05 * jax.random.normal(jax.random.fold_in(_tk, 500 + 28), (1000, 64), jnp.float32)
        tbl_29 = 0.05 * jax.random.normal(jax.random.fold_in(_tk, 500 + 29), (1000, 64), jnp.float32)
        tbl_30 = 0.05 * jax.random.normal(jax.random.fold_in(_tk, 500 + 30), (1000, 64), jnp.float32)
        tbl_31 = 0.05 * jax.random.normal(jax.random.fold_in(_tk, 500 + 31), (12500, 64), jnp.float32)
        tbl_32 = 0.05 * jax.random.normal(jax.random.fold_in(_tk, 500 + 32), (1000, 64), jnp.float32)
        tbl_33 = 0.05 * jax.random.normal(jax.random.fold_in(_tk, 500 + 33), (1250, 64), jnp.float32)
        tbl_34 = 0.05 * jax.random.normal(jax.random.fold_in(_tk, 500 + 34), (1250, 64), jnp.float32)
        tbl_35 = 0.05 * jax.random.normal(jax.random.fold_in(_tk, 500 + 35), (1000, 64), jnp.float32)
        tbl_36 = 0.05 * jax.random.normal(jax.random.fold_in(_tk, 500 + 36), (1250, 64), jnp.float32)
        tbl_37 = 0.05 * jax.random.normal(jax.random.fold_in(_tk, 500 + 37), (1000, 64), jnp.float32)
        tbl_38 = 0.05 * jax.random.normal(jax.random.fold_in(_tk, 500 + 38), (1000, 64), jnp.float32)
        _rk = jax.random.fold_in(_tk, 7)
        W_top1 = 0.0606339 * jax.random.normal(jax.random.fold_in(_tk, 801), (272, 512), jnp.float32)
        W_top2 = 0.0441942 * jax.random.normal(jax.random.fold_in(_tk, 802), (512, 256), jnp.float32)
        W_top3 = 0.0625 * jax.random.normal(jax.random.fold_in(_tk, 803), (256, 1), jnp.float32)
        b_top1 = jnp.zeros((512,), jnp.float32)
        b_top2 = jnp.zeros((256,), jnp.float32)
        return (dense_ctx, ids, tbl_0, tbl_1, tbl_2, tbl_3, tbl_4, tbl_5, tbl_6, tbl_7, tbl_8, tbl_9, tbl_10, tbl_11, tbl_12, tbl_13, tbl_14, tbl_15, tbl_16, tbl_17, tbl_18, tbl_19, tbl_20, tbl_21, tbl_22, tbl_23, tbl_24, tbl_25, tbl_26, tbl_27, tbl_28, tbl_29, tbl_30, tbl_31, tbl_32, tbl_33, tbl_34, tbl_35, tbl_36, tbl_37, tbl_38, W_top1, b_top1, W_top2, b_top2, W_top3)
    dense_ctx, ids, tbl_0, tbl_1, tbl_2, tbl_3, tbl_4, tbl_5, tbl_6, tbl_7, tbl_8, tbl_9, tbl_10, tbl_11, tbl_12, tbl_13, tbl_14, tbl_15, tbl_16, tbl_17, tbl_18, tbl_19, tbl_20, tbl_21, tbl_22, tbl_23, tbl_24, tbl_25, tbl_26, tbl_27, tbl_28, tbl_29, tbl_30, tbl_31, tbl_32, tbl_33, tbl_34, tbl_35, tbl_36, tbl_37, tbl_38, W_top1, b_top1, W_top2, b_top2, W_top3 = _rec_inputs()

    def _L0_rec_setup():
        import jax, jax.numpy as jnp
        import numpy as np
        key = jax.random.key(seed)
        k1, k2 = jax.random.split(key)
        B, F, E, O = (2048, 39, 64, 256)
        inputs = jax.random.normal(k1, (B, F, E), dtype=jnp.float32)
        p_weight = jax.random.normal(k2, (E * E, O), dtype=jnp.float32) * 0.01
        return {'inputs': inputs, 'p_weight': p_weight}
    _L0_rec_all = _L0_rec_setup()
    _L0_rec_in = {k: v for k, v in _L0_rec_all.items() if k in ('p_weight',)}
    del _L0_rec_all
    return {'dense_ctx': dense_ctx, 'ids': ids, 'tbl_0': tbl_0, 'tbl_1': tbl_1, 'tbl_2': tbl_2, 'tbl_3': tbl_3, 'tbl_4': tbl_4, 'tbl_5': tbl_5, 'tbl_6': tbl_6, 'tbl_7': tbl_7, 'tbl_8': tbl_8, 'tbl_9': tbl_9, 'tbl_10': tbl_10, 'tbl_11': tbl_11, 'tbl_12': tbl_12, 'tbl_13': tbl_13, 'tbl_14': tbl_14, 'tbl_15': tbl_15, 'tbl_16': tbl_16, 'tbl_17': tbl_17, 'tbl_18': tbl_18, 'tbl_19': tbl_19, 'tbl_20': tbl_20, 'tbl_21': tbl_21, 'tbl_22': tbl_22, 'tbl_23': tbl_23, 'tbl_24': tbl_24, 'tbl_25': tbl_25, 'tbl_26': tbl_26, 'tbl_27': tbl_27, 'tbl_28': tbl_28, 'tbl_29': tbl_29, 'tbl_30': tbl_30, 'tbl_31': tbl_31, 'tbl_32': tbl_32, 'tbl_33': tbl_33, 'tbl_34': tbl_34, 'tbl_35': tbl_35, 'tbl_36': tbl_36, 'tbl_37': tbl_37, 'tbl_38': tbl_38, 'W_top1': W_top1, 'b_top1': b_top1, 'W_top2': W_top2, 'b_top2': b_top2, 'W_top3': W_top3, 'L0_rec_p_weight': _L0_rec_in['p_weight']}

def reference(dense_ctx, ids, tbl_0, tbl_1, tbl_2, tbl_3, tbl_4, tbl_5, tbl_6, tbl_7, tbl_8, tbl_9, tbl_10, tbl_11, tbl_12, tbl_13, tbl_14, tbl_15, tbl_16, tbl_17, tbl_18, tbl_19, tbl_20, tbl_21, tbl_22, tbl_23, tbl_24, tbl_25, tbl_26, tbl_27, tbl_28, tbl_29, tbl_30, tbl_31, tbl_32, tbl_33, tbl_34, tbl_35, tbl_36, tbl_37, tbl_38, W_top1, b_top1, W_top2, b_top2, W_top3, L0_rec_p_weight):
    import jax
    import jax.numpy as jnp

    def _L0_rec_ref(inputs, p_weight):
        import jax, jax.numpy as jnp
        import numpy as np
        B, F, E = inputs.shape
        f_sigma = jnp.sum(inputs, axis=1)
        p = (f_sigma[:, :, None] * f_sigma[:, None, :]).reshape(B, E * E)
        return p @ p_weight
    e = jnp.stack([tbl_0[ids[:, 0]], tbl_1[ids[:, 1]], tbl_2[ids[:, 2]], tbl_3[ids[:, 3]], tbl_4[ids[:, 4]], tbl_5[ids[:, 5]], tbl_6[ids[:, 6]], tbl_7[ids[:, 7]], tbl_8[ids[:, 8]], tbl_9[ids[:, 9]], tbl_10[ids[:, 10]], tbl_11[ids[:, 11]], tbl_12[ids[:, 12]], tbl_13[ids[:, 13]], tbl_14[ids[:, 14]], tbl_15[ids[:, 15]], tbl_16[ids[:, 16]], tbl_17[ids[:, 17]], tbl_18[ids[:, 18]], tbl_19[ids[:, 19]], tbl_20[ids[:, 20]], tbl_21[ids[:, 21]], tbl_22[ids[:, 22]], tbl_23[ids[:, 23]], tbl_24[ids[:, 24]], tbl_25[ids[:, 25]], tbl_26[ids[:, 26]], tbl_27[ids[:, 27]], tbl_28[ids[:, 28]], tbl_29[ids[:, 29]], tbl_30[ids[:, 30]], tbl_31[ids[:, 31]], tbl_32[ids[:, 32]], tbl_33[ids[:, 33]], tbl_34[ids[:, 34]], tbl_35[ids[:, 35]], tbl_36[ids[:, 36]], tbl_37[ids[:, 37]], tbl_38[ids[:, 38]]], axis=1)
    z = _L0_rec_ref(e, L0_rec_p_weight)
    z = z.reshape(z.shape[0], -1)
    h = jnp.concatenate([z, dense_ctx], axis=1)
    h = jnp.maximum(h @ W_top1 + b_top1, 0.0)
    h = jnp.maximum(h @ W_top2 + b_top2, 0.0)
    y = h @ W_top3
    return y

_drawn_inputs = setup_inputs


def setup_inputs(seed=0):
    import zlib

    import numpy as np

    out = dict(_drawn_inputs(seed))
    spreads = {'b_top1': (0.0, 0.1), 'b_top2': (0.0, 0.1)}
    factors = {}
    for name, (base, spread) in spreads.items():
        noise = np.random.default_rng([zlib.crc32(name.encode()), seed]).standard_normal(out[name].shape)
        drawn = base * np.exp(spread * noise) if base else spread * noise
        out[name] = jnp.asarray(drawn.astype(out[name].dtype))
    for name, factor in factors.items():
        out[name] = (out[name] * factor).astype(out[name].dtype)
    return out
```

```python
import concourse.bass as bass
from concourse import mybir
from contextlib import ExitStack

BATCH = 2048
EMB = 64
OUTER = 256
HID1 = 512
HID2 = 256
DENSE = 16
P = 128

TILES = BATCH // P
CHUNK_TILES = 4
CHUNKS = TILES // CHUNK_TILES
CB = CHUNK_TILES * P
ROWS_P = 125

SMALL_J, MID_J = 8, 10
N_SMALL, N_MID = 16, 2
N_HOT = N_SMALL + N_MID
HALF = N_SMALL // 2
SEGMENTS = [(0, HALF, SMALL_J), (HALF, HALF, SMALL_J), (N_SMALL, N_MID, MID_J)]
KT_CHUNK = N_SMALL * SMALL_J + N_MID * MID_J
BUILT = [sum(n * j for _, n, j in SEGMENTS[:g]) for g in range(len(SEGMENTS))]
PARTS = 3
SLOTS = MID_J
AHEAD = SMALL_J
ROTS = EMB // 2
PAIR_TILES = ROTS // 2 + 1
TURN = ROTS // 2
WRAP = EMB - 2 * TURN + 1
PRODS = 3


def split_tables(rows):
    small = [f for f, r in enumerate(rows) if r == SMALL_J * ROWS_P][:N_SMALL]
    mid = [f for f, r in enumerate(rows) if r == MID_J * ROWS_P][:N_MID]
    hot = small + mid
    return hot, [f for f in range(len(rows)) if f not in hot]


def tower(nc, dense_ctx, ids, tables, w1, b1, w2, b2, w3, w_pair, eye, row_of, out):
    fp32, bf16, fp16, i32 = mybir.dt.float32, mybir.dt.bfloat16, mybir.dt.float16, mybir.dt.int32
    ALU = mybir.AluOpType
    ACT = mybir.ActivationFunctionType
    AX = mybir.AxisListType
    FIELDS = len(tables)
    hot, cold = split_tables([t.shape[0] for t in tables])
    COLD = len(cold)
    J = [SMALL_J] * N_SMALL + [MID_J] * N_MID

    ids_rows = nc.dram_tensor("ids_rows", (CHUNKS, N_HOT, CB), fp16)
    around = nc.dram_tensor("around", (2, EMB - WRAP, 2 * TURN, OUTER), fp32)

    with ExitStack() as ctx:
        def sb(name, shape, dt):
            return ctx.enter_context(nc.sbuf_tensor(name, shape, dt))

        def ps(name, shape):
            return ctx.enter_context(nc.psum_tensor(name, shape, fp32))

        def sem(name):
            return ctx.enter_context(nc.semaphore(name))

        ids_sb = sb("ids_sb", [P, TILES, FIELDS], i32)
        index = sb("index", [P, 2 * CHUNK_TILES, FIELDS], i32)
        ids_hot = sb("ids_hot", [P, TILES, N_HOT], fp16)
        ids_bc = sb("ids_bc", [P, N_HOT * CB], fp16)
        eye_sb = sb("eye_sb", [P, P], fp32)
        eye_h = sb("eye_h", [P, P], fp16)
        row_sb = sb("row_sb", [P, SMALL_J + MID_J], fp32)
        early = sb("early", [P, 4 * MID_J * EMB], fp32)
        stage = early[:, 0:2 * MID_J * EMB].rearrange("p (h x) -> p h x", h=2)
        rest = early[:, 2 * MID_J * EMB:].rearrange("p (h x) -> p h x", h=2)
        prod = early[:, 0:PRODS * CB].rearrange("p (k b) -> p k b", k=PRODS)
        s_rep = early[:, PRODS * CB:(PRODS + 1) * CB]
        parts = sb("parts", [P, KT_CHUNK * PARTS * EMB], bf16)
        gathered = sb("gathered", [P, 2 * CHUNK_TILES, COLD, EMB], fp32)
        onehot = sb("onehot", [P, SLOTS, CB], bf16)
        ids_t = sb("ids_t", [N_HOT, TILES * P], fp16)
        wa = sb("wa", [P, PAIR_TILES, OUTER], fp32)
        late = sb("late", [P, PAIR_TILES * OUTER], fp32)
        wb = late[:, :].rearrange("p (k o) -> p k o", k=PAIR_TILES)
        z_sb = late[:, 0:2 * CB].rearrange("p (m b) -> p m b", m=2)
        h1_sb = late[:, 2 * CB:6 * CB].rearrange("p (m b) -> p m b", m=4)
        h2_sb = late[:, 6 * CB:8 * CB].rearrange("p (m b) -> p m b", m=2)
        w1_sb = sb("w1_sb", [P, OUTER // P, HID1], fp32)
        w1d_sb = sb("w1d_sb", [DENSE, HID1], fp32)
        w2_sb = sb("w2_sb", [P, HID1 // P, HID2], fp32)
        w3_sb = sb("w3_sb", [P, HID2 // P], fp32)
        b1_sb = sb("b1_sb", [P, HID1 // P], fp32)
        b2_sb = sb("b2_sb", [P, HID2 // P], fp32)
        dense_sb = sb("dense_sb", [P, TILES, DENSE], fp32)
        dense_t = sb("dense_t", [DENSE, TILES * P], fp32)
        hot_sum = sb("hot_sum", [P, CHUNK_TILES, EMB], fp32)
        cold_sum = sb("cold_sum", [P, CHUNK_TILES, EMB], fp32)
        s_ext = sb("s_ext", [P, CHUNK_TILES, 3, EMB], fp32)
        s_row = s_ext[:, :, :, :].rearrange("p t c e -> p t (c e)")
        y_sb = sb("y_sb", [P, TILES], fp32)

        acc_ps = ps("acc_ps", [P, 4, 512])
        rot_ps = ps("rot_ps", [P, 2, 512])
        z_ps = ps("z_ps", [P, 2, 512])

        ids_landed = sem("ids_landed")
        index_landed = [sem(f"index_landed{i}") for i in range(2 * CHUNK_TILES)]
        const_landed = sem("const_landed")
        table_landed = [sem(f"table_landed{i}") for i in range(2)]
        weight_landed = sem("weight_landed")
        around_landed = sem("around_landed")
        pair_w_landed = sem("pair_w_landed")
        tile_landed = [sem(f"tile_landed{i}") for i in range(2 * CHUNK_TILES)]
        tiles_begun = sem("tiles_begun")
        out_landed = sem("out_landed")
        ids_hot_ready = sem("ids_hot_ready")
        eye_h_ready = sem("eye_h_ready")
        ids_tr = sem("ids_tr")
        ids_t_ready = sem("ids_t_ready")
        ids_stored = sem("ids_stored")
        ids_bc_landed = [sem(f"ids_bc_landed{i}") for i in range(2)]
        hi_ready = sem("hi_ready")
        rest_ready = sem("rest_ready")
        mid_ready = sem("mid_ready")
        lo_ready = sem("lo_ready")
        dense_tr = sem("dense_tr")
        dense_ready = sem("dense_ready")
        hot_ready = sem("hot_ready")
        hot_free = sem("hot_free")
        wb_cleared = sem("wb_cleared")
        pair_w_ready = sem("pair_w_ready")
        hot_summed = sem("hot_summed")
        slot_free = sem("slot_free")
        s_ready = sem("s_ready")
        rep_done = sem("rep_done")
        rep_copied = sem("rep_copied")
        rot_done = sem("rot_done")
        prod_ready = sem("prod_ready")
        prod_used = sem("prod_used")
        z_copied = sem("z_copied")
        h1_done = sem("h1_done")
        h1_ready = sem("h1_ready")
        h2_done = sem("h2_done")
        h2_ready = sem("h2_ready")
        y_done = sem("y_done")
        y_copied = sem("y_copied")

        COPIES = [[CHUNK_TILES * EMB, P], [0, 3], [1, EMB]]
        PAIR_LOADS = 2 * (2 * 3 + 1)

        block = ctx.enter_context(nc.Block())

        def segment_pairs(eng, g):
            first, n, j = SEGMENTS[g]
            return eng.Fori(0, n // 2), first, j

        @block.sync
        def _(sp):
            ids_tiles = ids.rearrange("(p t) f -> p t f", p=P)
            sp.dma_start(index[:, 0, :], ids_tiles[:, 0, :]).then_inc(index_landed[0], 16)
            sp.dma_start(ids_sb[:, :, :], ids_tiles).then_inc(ids_landed, 16)
            sp.dma_start(eye_sb[:, :], eye).then_inc(const_landed, 16)
            sp.dma_start(row_sb[:, :], row_of).then_inc(const_landed, 16)
            sp.dma_start(index[:, 1, :], ids_tiles[:, 1, :]).then_inc(index_landed[1], 16)

            def load_table(n):
                sp.dma_start(stage[0:ROWS_P, n % 2, 0:J[n] * EMB],
                             tables[hot[n]].rearrange("(p j) e -> p (j e)", j=J[n])).then_inc(table_landed[n % 2], 16)

            load_table(0)
            load_table(1)
            sp.dma_start(dense_sb[:, :, :], dense_ctx.rearrange("(p t) f -> p t f", p=P)).then_inc(const_landed, 16)
            for u in range(2, 2 * CHUNK_TILES):
                sp.dma_start(index[:, u, :], ids_tiles[:, u, :]).then_inc(index_landed[u], 16)

            steps = [(EMB, 1), (1, EMB)]
            for a, (step_i, step_j) in enumerate(steps):
                for half, j in enumerate((EMB - TURN, 0)):
                    src = bass.AP(w_pair.tensor, (WRAP * step_i + j * step_j) * OUTER,
                                  [[step_i * OUTER, EMB - WRAP], [step_j * OUTER, TURN], [1, OUTER]])
                    sp.dma_start(around[a, :, half * TURN:(half + 1) * TURN, :], src).then_inc(around_landed, 16)

            for n in range(2, N_HOT):
                sp.wait_ge(rest_ready, n - 1)
                load_table(n)

            sp.wait_ge(wb_cleared, 1)
            for a, (dst, (step_i, step_j)) in enumerate(zip((wa, wb), steps)):
                for at, i, n, j, k0 in (
                    (0, 0, WRAP, TURN, 0),
                    (EMB - TURN, EMB - TURN, TURN, 0, 0),
                    (EMB, TURN, WRAP, TURN, a),
                    (P - TURN, 0, TURN, 0, a),
                ):
                    src = bass.AP(w_pair.tensor, (i * step_i + (j + k0) * step_j) * OUTER,
                                  [[(step_i + step_j) * OUTER, n], [step_j * OUTER, TURN - k0], [1, OUTER]])
                    sp.dma_start(dst[at:at + n, k0:TURN, :], src).then_inc(pair_w_landed, 16)
                src = bass.AP(w_pair.tensor, ROTS * step_j * OUTER, [[(step_i + step_j) * OUTER, ROTS], [1, OUTER]])
                sp.dma_start(dst[0:ROTS, TURN, :], src).then_inc(pair_w_landed, 16)
            sp.wait_ge(around_landed, 16 * 4)
            for a, dst in enumerate((wa, wb)):
                for at, i, j, k0 in ((WRAP, WRAP, WRAP + TURN, 0), (EMB + WRAP, WRAP + TURN, WRAP + TURN, a)):
                    src = bass.AP(around, ((a * (EMB - WRAP) + i - WRAP) * 2 * TURN + j + k0 - (EMB - TURN)) * OUTER,
                                  [[(2 * TURN + 1) * OUTER, TURN - 1], [OUTER, TURN - k0], [1, OUTER]])
                    sp.dma_start(dst[at:at + TURN - 1, k0:TURN, :], src).then_inc(pair_w_landed, 16)

            with sp.Fori(1, CHUNKS // 2) as pair:
                for u in range(2 * CHUNK_TILES):
                    sp.wait_ge(tile_landed[u], pair * (16 * COLD))
                    sp.dma_start(index[:, u, :], ids_tiles[:, bass.ds(pair * (2 * CHUNK_TILES) + u, 1), :]
                                 .rearrange("p t f -> p (t f)")).then_inc(index_landed[u], 16)
            sp.wait_ge(y_copied, CHUNKS)
            sp.dma_start(out.rearrange("(p t) o -> p (t o)", p=P), y_sb[:, :]).then_inc(out_landed, 16)
            sp.wait_ge(out_landed, 16)

        @block.gpsimd
        def _(pool):
            with pool.Fori(0, CHUNKS // 2) as pair:
                for u in range(2 * CHUNK_TILES):
                    pool.wait_ge(index_landed[u], (pair + 1) * 16)
                    pool.wait_ge(slot_free, pair * (2 * CHUNK_TILES) + u + 1)
                    pool.sem_inc(tiles_begun, 1)
                    for g, f in enumerate(cold):
                        nc.gpsimd.indirect_dma_start(
                            out=gathered[:, u, g, :], out_offset=None, in_=tables[f],
                            in_offset=bass.IndirectOffsetOnAxis(ap=index[:, u, f:f + 1], axis=0),
                        ).then_inc(tile_landed[u], 16)

        @block.scalar
        def _(act):
            act.wait_ge(ids_tr, 1)
            nc.scalar.activation(ids_t[:, :], z_ps[0:N_HOT, :, :].rearrange("p m b -> p (m b)").bitcast(fp16),
                                 ACT.Copy).then_inc(ids_t_ready, 1)
            act.wait_ge(ids_t_ready, 1)
            act.dma_start(ids_rows[:, :, :].rearrange("c n b -> n c b"),
                          ids_t[:, :].rearrange("n (c b) -> n c b", b=CB)).then_inc(ids_stored, 16)

            def load_ids(c, part):
                first, n = ((0, HALF), (HALF, N_HOT - HALF))[part]
                if c:
                    act.wait_ge(hot_ready, (c - 1) * KT_CHUNK + (BUILT[1], KT_CHUNK)[part])
                src = bass.AP(ids_rows, (c * N_HOT + first) * CB, [[0, P], [1, n * CB]])
                act.dma_start(ids_bc[:, first * CB:(first + n) * CB], src).then_inc(ids_bc_landed[part], 16)

            def part_of(kt, j, s):
                return parts[0:ROWS_P, bass.ds(kt * (PARTS * EMB), j * PARTS * EMB)]\
                    .rearrange("p (j s e) -> p j s e", s=PARTS, e=EMB)[:, :, s, :]

            def split(g):
                loop, first, j = segment_pairs(act, g)
                with loop as m:
                    for h in range(2):
                        kt = m * (2 * j) + (BUILT[g] + h * j)
                        act.wait_ge(table_landed[h], m * 16 + (first // 2 + 1) * 16)
                        nc.scalar.activation(part_of(kt, j, 0), stage[0:ROWS_P, h, 0:j * EMB]
                                             .rearrange("p (j e) -> p j e", e=EMB), ACT.Copy).then_inc(hi_ready, 1)
                    for h in range(2):
                        kt = m * (2 * j) + (BUILT[g] + h * j)
                        act.wait_ge(rest_ready, m * 2 + (first + h + 1))
                        nc.scalar.activation(part_of(kt, j, 1), rest[0:ROWS_P, h, 0:j * EMB]
                                             .rearrange("p (j e) -> p j e", e=EMB), ACT.Copy).then_inc(mid_ready, 1)

            act.wait_ge(ids_stored, 16)
            load_ids(0, 0)
            load_ids(0, 1)
            split(0)
            load_ids(1, 0)
            for g in (1, 2):
                split(g)
            act.dma_start(w1_sb[:, :, :], w1[0:OUTER, :].rearrange("(k p) m -> p k m", p=P)).then_inc(weight_landed, 16)
            act.dma_start(w1d_sb[:, :], w1[OUTER:OUTER + DENSE, :]).then_inc(weight_landed, 16)
            act.dma_start(w2_sb[:, :, :], w2.rearrange("(k p) m -> p k m", p=P)).then_inc(weight_landed, 16)
            with nc.allow_non_contiguous_dma(reason="a few hundred single elements"):
                act.dma_start(w3_sb[:, :], w3.rearrange("(k p) o -> p (k o)", p=P)).then_inc(weight_landed, 16)
                act.dma_start(b1_sb[:, :], b1.rearrange("(k p) -> p k", p=P)).then_inc(weight_landed, 16)
                act.dma_start(b2_sb[:, :], b2.rearrange("(k p) -> p k", p=P)).then_inc(weight_landed, 16)
            load_ids(1, 1)

            def hidden1(c):
                for m in range(4):
                    act.wait_ge(h1_done, 4 * c + m + 1)
                    nc.scalar.activation(h1_sb[:, m, :], z_ps[:, m % 2, :], ACT.Relu, bias=b1_sb[:, m:m + 1])\
                        .then_inc(h1_ready, 1)

            def hidden2(c):
                for m in range(2):
                    act.wait_ge(h2_done, 2 * c + m + 1)
                    nc.scalar.activation(h2_sb[:, m, :], z_ps[:, m, :], ACT.Relu, bias=b2_sb[:, m:m + 1])\
                        .then_inc(h2_ready, 1)

            def output(c):
                act.wait_ge(y_done, c + 1)
                nc.scalar.activation(y_sb[:, c * CHUNK_TILES:(c + 1) * CHUNK_TILES],
                                     acc_ps[:, 2 * ((c + 1) % 2), 0:CHUNK_TILES], ACT.Copy).then_inc(y_copied, 1)

            act.wait_ge(weight_landed, 16 * 6)
            for c in range(CHUNKS):
                if c + 2 < CHUNKS:
                    load_ids(c + 2, 0)
                    load_ids(c + 2, 1)
                if c == 0:
                    for q in range(CHUNKS):
                        act.wait_ge(dense_tr, q + 1)
                        nc.scalar.activation(dense_t[:, q * CB:(q + 1) * CB], z_ps[0:DENSE, q % 2, :], ACT.Copy)\
                            .then_inc(dense_ready, 1)
                if c:
                    hidden1(c - 1)
                act.wait_ge(rep_done, c + 1)
                nc.scalar.activation(s_rep[0:EMB, :], rot_ps[0:EMB, 1, :], ACT.Copy)
                act.wait_ge(rot_done, c * PAIR_TILES + 1)
                nc.scalar.activation(s_rep[EMB:P, :], rot_ps[EMB:P, 0, :], ACT.Copy).then_inc(rep_copied, 1)
                if c:
                    hidden2(c - 1)
                    output(c - 1)
                act.wait_ge(prod_used, (c + 1) * PAIR_TILES)
                for m in range(2):
                    nc.scalar.activation(z_sb[:, m, :], z_ps[:, m, :], ACT.Copy).then_inc(z_copied, 1)
            hidden1(CHUNKS - 1)
            hidden2(CHUNKS - 1)
            output(CHUNKS - 1)

        @block.vector
        def _(dve):
            dve.sem_inc(slot_free, 2 * CHUNK_TILES)
            nc.vector.memset(wb[EMB:P, 0, :], 0.0).then_inc(wb_cleared, 1)
            dve.wait_ge(ids_landed, 16)
            for n, f in enumerate(hot):
                last = nc.vector.tensor_copy(ids_hot[:, :, n], ids_sb[:, :, f])
            last.then_inc(ids_hot_ready, 1)
            dve.wait_ge(const_landed, 16 * 3)
            nc.vector.tensor_copy(eye_h[:, :], eye_sb[:, :]).then_inc(eye_h_ready, 1)

            def remainders(g, m, j, first):
                def operands(h):
                    kt = m * (2 * j) + (BUILT[g] + h * j)
                    whole = parts[0:ROWS_P, bass.ds(kt * (PARTS * EMB), j * PARTS * EMB)]\
                        .rearrange("p (j s e) -> p j s e", s=PARTS, e=EMB)
                    return whole, *(x[0:ROWS_P, h, 0:j * EMB].rearrange("p (j e) -> p j e", e=EMB)
                                    for x in (stage, rest))

                for h in range(2):
                    whole, st, r = operands(h)
                    dve.wait_ge(hi_ready, m * 2 + (first + h + 1))
                    nc.vector.tensor_tensor(r, st, whole[:, :, 0, :], ALU.subtract).then_inc(rest_ready, 1)
                for h in range(2):
                    whole, st, r = operands(h)
                    dve.wait_ge(rest_ready, m * 2 + (first + h + 1))
                    dve.wait_ge(mid_ready, m * 2 + (first + h + 1))
                    nc.vector.tensor_tensor(whole[:, :, 2, :], r, whole[:, :, 1, :], ALU.subtract).then_inc(lo_ready, 1)

            def sums(c):
                dve.wait_ge(hot_free, (c + 1) * KT_CHUNK + AHEAD)
                for b in range(2):
                    last = nc.vector.tensor_reduce(
                        hot_sum[:, 2 * b:2 * b + 2, :],
                        acc_ps[:, 2 * (c % 2) + b, 0:2 * PARTS * EMB].rearrange("p (t s e) -> p t e s", t=2, s=PARTS),
                        AX.X, ALU.add)
                last.then_inc(hot_summed, 1)
                for u in range(CHUNK_TILES):
                    slot = c % 2 * CHUNK_TILES + u
                    dve.wait_ge(tile_landed[slot], (c // 2 + 1) * 16 * COLD)
                    nc.vector.tensor_reduce(cold_sum[:, u, :], gathered[:, slot, :, :].rearrange("p g e -> p e g"),
                                            AX.X, ALU.add).then_inc(slot_free, 1)
                    dve.wait_ge(slot_free, c * CHUNK_TILES + 2 * CHUNK_TILES + u + 1)
                    dve.wait_ge(hot_summed, c + 1)
                    nc.vector.tensor_tensor(s_ext[:, u, :, :], bass.AP(cold_sum, u * EMB, COPIES),
                                            bass.AP(hot_sum, u * EMB, COPIES), ALU.add).then_inc(s_ready, 1)

            def build(c):
                for g in range(len(SEGMENTS)):
                    loop, first, j_count = segment_pairs(dve, g)
                    if g < 2:
                        dve.wait_ge(ids_bc_landed[g], 16 * (c + 1))
                    if g == 2 and c == 1:
                        sums(0)
                    with loop as m:
                        if c == 0:
                            remainders(g, m, j_count, first)
                        for h in range(2):
                            for j in range(j_count):
                                dve.wait_ge(hot_free, m * (2 * j_count) + (c * KT_CHUNK + BUILT[g] + h * j_count + j + 1))
                                nc.vector.tensor_scalar(
                                    onehot[0:ROWS_P, j, :],
                                    ids_bc[0:ROWS_P, bass.ds(m * (2 * CB) + (first + h) * CB, CB)],
                                    row_sb[0:ROWS_P, (j_count - SMALL_J) * SMALL_J // 2 + j:
                                           (j_count - SMALL_J) * SMALL_J // 2 + j + 1],
                                    None, ALU.is_equal).then_inc(hot_ready, 1)

            def products(c):
                dve.wait_ge(rep_copied, c + 1)
                for k in range(PAIR_TILES):
                    rows = P if k < PAIR_TILES - 1 else ROTS
                    dve.wait_ge(rot_done, c * PAIR_TILES + k + 1)
                    if c * PAIR_TILES + k >= PRODS:
                        dve.wait_ge(prod_used, c * PAIR_TILES + k + 1 - PRODS)
                    nc.vector.tensor_tensor(prod[0:rows, k % PRODS, :], rot_ps[0:rows, k % 2, :],
                                            s_rep[0:rows, :], ALU.mult).then_inc(prod_ready, 1)

            build(0)
            for c in range(CHUNKS):
                if c + 1 < CHUNKS:
                    build(c + 1)
                if c == 0:
                    dve.wait_ge(pair_w_landed, 16 * PAIR_LOADS)
                    nc.vector.tensor_tensor(wa[:, 0:TURN, :], wa[:, 0:TURN, :], wb[:, 0:TURN, :], ALU.add)
                    nc.vector.tensor_tensor(wa[0:ROTS, TURN, :], wa[0:ROTS, TURN, :], wb[0:ROTS, TURN, :], ALU.add)\
                        .then_inc(pair_w_ready, 1)
                if c:
                    sums(c)
                products(c)

        @block.tensor
        def _(pe):
            pe.sem_inc(hot_free, AHEAD)
            pe.wait_ge(ids_hot_ready, 1)
            pe.wait_ge(eye_h_ready, 1)
            ids_ps = z_ps[0:N_HOT, :, :].rearrange("p m b -> p (m b)").bitcast(fp16)
            for t in range(TILES):
                last = nc.tensor.transpose(ids_ps[:, t * P:(t + 1) * P], ids_hot[:, t, :], eye_h[:, :])
            last.then_inc(ids_tr, 1)

            def look_up(c):
                for g in range(len(SEGMENTS)):
                    first, n, j_count = SEGMENTS[g]

                    def pair_of_tables(m, begin):
                        for h in range(2):
                            if c == 0:
                                pe.wait_ge(lo_ready, m * 2 + (first + h + 1))
                            for j in range(j_count):
                                kt = m * (2 * j_count) + (BUILT[g] + h * j_count + j)
                                pe.wait_ge(hot_ready, kt + (c * KT_CHUNK + 1))
                                for u in range(CHUNK_TILES):
                                    at = (u % 2) * PARTS * EMB
                                    last = nc.tensor.matmul(
                                        acc_ps[:, 2 * (c % 2) + u // 2, at:at + PARTS * EMB],
                                        onehot[0:ROWS_P, j, u * P:(u + 1) * P],
                                        parts[0:ROWS_P, bass.ds(kt * (PARTS * EMB), PARTS * EMB)],
                                        start=begin and h == 0 and j == 0 and u % 2 == 0, stop=False,
                                        skip_group_check=True)
                                last.then_inc(hot_free, 1)

                    if g == 0:
                        pair_of_tables(0, True)
                    with pe.Fori(1 if g == 0 else 0, n // 2) as m:
                        pair_of_tables(m, False)

            def rotate(bank, turn, rows, signal):
                for u in range(CHUNK_TILES):
                    last = nc.tensor.transpose(rot_ps[0:rows, bank, u * P:(u + 1) * P],
                                               s_row[:, u, turn:turn + rows], eye_sb[:, :])
                last.then_inc(signal, 1)

            def rotate_tile(k):
                rotate(k % 2, TURN + k, P if k < PAIR_TILES - 1 else ROTS, rot_done)

            def hidden1(c):
                for m in range(4):
                    pe.wait_ge(z_copied, 2 * c + 2)
                    if m >= 2:
                        pe.wait_ge(h1_ready, 4 * c + m - 1)
                    nc.tensor.matmul(z_ps[:, m % 2, :], w1d_sb[:, m * P:(m + 1) * P], dense_t[:, c * CB:(c + 1) * CB],
                                     start=True, stop=False)
                    for k in range(2):
                        last = nc.tensor.matmul(z_ps[:, m % 2, :], w1_sb[:, k, m * P:(m + 1) * P], z_sb[:, k, :],
                                                start=False, stop=k == 1)
                    last.then_inc(h1_done, 1)

            def hidden2(c):
                for m in range(2):
                    for k in range(4):
                        pe.wait_ge(h1_ready, 4 * c + max(k + 1, 3 + m))
                        last = nc.tensor.matmul(z_ps[:, m, :], w2_sb[:, k, m * P:(m + 1) * P], h1_sb[:, k, :],
                                                start=k == 0, stop=k == 3)
                    last.then_inc(h2_done, 1)

            def output(c):
                pe.wait_ge(h2_ready, 2 * c + 2)
                for u in range(CHUNK_TILES):
                    for k in range(2):
                        last = nc.tensor.matmul(acc_ps[:, 2 * ((c + 1) % 2), u:u + 1], h2_sb[:, k, u * P:(u + 1) * P],
                                                w3_sb[:, k:k + 1], start=k == 0, stop=k == 1)
                last.then_inc(y_done, 1)

            look_up(0)
            for c in range(CHUNKS):
                if c + 1 < CHUNKS:
                    if c >= 2:
                        pe.wait_ge(y_copied, c - 1)
                    look_up(c + 1)
                if c == 0:
                    pe.wait_ge(ids_t_ready, 1)
                    for q in range(CHUNKS):
                        if q >= 2:
                            pe.wait_ge(dense_ready, q - 1)
                        for u in range(CHUNK_TILES):
                            last = nc.tensor.transpose(z_ps[0:DENSE, q % 2, u * P:(u + 1) * P],
                                                       dense_sb[:, q * CHUNK_TILES + u, :], eye_sb[:, :])
                        last.then_inc(dense_tr, 1)
                if c:
                    hidden1(c - 1)
                pe.wait_ge(s_ready, (c + 1) * CHUNK_TILES)
                rotate(1, 0, P, rep_done)
                rotate_tile(0)
                if c:
                    hidden2(c - 1)
                pe.wait_ge(rep_copied, c + 1)
                rotate_tile(1)
                if c:
                    output(c - 1)
                else:
                    pe.wait_ge(dense_ready, CHUNKS)
                    pe.wait_ge(pair_w_ready, 1)
                for k in range(PAIR_TILES):
                    rows = P if k < PAIR_TILES - 1 else ROTS
                    pe.wait_ge(prod_ready, c * PAIR_TILES + k + 1)
                    for m in range(2):
                        last = nc.tensor.matmul(z_ps[:, m, :], wa[0:rows, k, m * P:(m + 1) * P],
                                                prod[0:rows, k % PRODS, :], start=k == 0, stop=k == PAIR_TILES - 1)
                    last.then_inc(prod_used, 1)
                    if k + 2 < PAIR_TILES:
                        rotate_tile(k + 2)
            hidden1(CHUNKS - 1)
            hidden2(CHUNKS - 1)
            output(CHUNKS - 1)


_FIELDS = 39
_TABLES = [f"tbl_{f}" for f in range(_FIELDS)]
_INS = ["dense_ctx", "ids"] + _TABLES + ["W_top1", "b_top1", "W_top2", "b_top2", "W_top3", "L0_rec_p_weight"]


def kernel(**inputs):
    import numpy as np
    import concourse.bacc as bacc
    from concourse.bass_utils import run_bass_kernel_spmd

    arrays = {f"in_{name}": np.ascontiguousarray(inputs[name]) for name in _INS}
    arrays["in_eye"] = np.eye(P, dtype=np.float32)
    lane = np.arange(P)[:, None]
    arrays["in_row_of"] = np.concatenate(
        [lane * j + np.arange(j)[None, :] for j in (SMALL_J, MID_J)], axis=1).astype(np.float32)

    nc = bacc.Bacc("TRN2", target_bir_lowering=False, num_devices=1)
    ap = {name: nc.dram_tensor(name, a.shape, mybir.dt.from_np(a.dtype), kind="ExternalInput").ap()
          for name, a in arrays.items()}
    y = nc.dram_tensor("y", (BATCH, 1), mybir.dt.float32, kind="ExternalOutput").ap()
    tower(nc, ap["in_dense_ctx"], ap["in_ids"], [ap[f"in_{t}"] for t in _TABLES], ap["in_W_top1"], ap["in_b_top1"],
          ap["in_W_top2"], ap["in_b_top2"], ap["in_W_top3"], ap["in_L0_rec_p_weight"], ap["in_eye"], ap["in_row_of"], y)
    return run_bass_kernel_spmd(nc, [arrays], core_ids=[0]).results[0]["y"]
```

```python
import concourse.bass as bass
from concourse import mybir
from contextlib import ExitStack

BATCH = 2048
EMB = 64
OUTER = 256
HID1 = 512
HID2 = 256
DENSE = 16
P = 128

TILES = BATCH // P
CHUNK_TILES = 4
CHUNKS = TILES // CHUNK_TILES
CB = CHUNK_TILES * P
GATHER_SLOTS = 8
ROWS_P = 125

SMALL_J, MID_J = 8, 10
N_SMALL, N_MID = 16, 4
N_HOT = N_SMALL + N_MID
N_FIRST = 12
SEGMENTS = [(0, N_FIRST, SMALL_J), (N_FIRST, N_SMALL - N_FIRST, SMALL_J), (N_SMALL, N_MID, MID_J)]
BUILT = [0, N_FIRST * SMALL_J, N_SMALL * SMALL_J]
J = [SMALL_J] * N_SMALL + [MID_J] * N_MID
START = [sum(J[:n]) for n in range(N_HOT)]
KT = sum(J)
SLOTS = 4
NARROW = 2

ROTS = EMB // 2
TURN = ROTS // 2
PAIR_TILES = ROTS // 2
PRODS = 3
SPAN = PAIR_TILES + P


def split_tables(rows):
    small = [f for f, r in enumerate(rows) if r == SMALL_J * ROWS_P][:N_SMALL]
    mid = [f for f, r in enumerate(rows) if r == MID_J * ROWS_P][:N_MID]
    hot = small + mid
    return hot, [f for f in range(len(rows)) if f not in hot]


def tower(nc, dense_t, ids, ids_hot, tables, w1, b1, w2, b2, w3, pair_a, pair_b, eye, fold_of, turns, row_of, out):
    fp32, bf16, fp16, i32 = mybir.dt.float32, mybir.dt.bfloat16, mybir.dt.float16, mybir.dt.int32
    fp32r = mybir.dt.float32r
    ALU = mybir.AluOpType
    ACT = mybir.ActivationFunctionType
    AX = mybir.AxisListType
    FIELDS = len(tables)
    hot, cold = split_tables([t.shape[0] for t in tables])
    COLD = len(cold)
    FLAT = N_HOT * BATCH // P

    ids_rows = nc.dram_tensor("ids_rows", (N_HOT, BATCH), fp16)

    with ExitStack() as ctx:
        def sb(name, shape, dt):
            return ctx.enter_context(nc.sbuf_tensor(name, shape, dt))

        def ps(name, shape):
            return ctx.enter_context(nc.psum_tensor(name, shape, fp32))

        def sem(name):
            return ctx.enter_context(nc.semaphore(name))

        index = sb("index", [P, GATHER_SLOTS, FIELDS], i32)
        gathered = sb("gathered", [P, GATHER_SLOTS, COLD, EMB], fp32)
        cold_sum = sb("cold_sum", [P, TILES, EMB], fp32)
        ids_raw = sb("ids_raw", [P, FLAT], i32)
        ids_h = sb("ids_h", [P, FLAT], fp16)
        ids_bc = sb("ids_bc", [P, 2, BATCH], fp16)
        eye_sb = sb("eye_sb", [P, P], fp32)
        fold_sb = sb("fold_sb", [P, P], fp32)
        turn_sb = sb("turn_sb", [P, SPAN + P], fp32)
        turn_r = sb("turn_r", [P, SPAN + P], fp32r)
        row_sb = sb("row_sb", [P, SMALL_J + MID_J], fp32)
        stage = sb("stage", [P, 2, MID_J * EMB], fp32)
        halves = sb("halves", [P, 2, MID_J, 2 * EMB], fp32r)
        onehot = sb("onehot", [P, SLOTS, BATCH], fp32r)
        narrow = sb("narrow", [P, NARROW, BATCH], bf16)
        wa = sb("wa", [P, PAIR_TILES + 1, OUTER], fp32)
        late = sb("late", [P, (PAIR_TILES + 1) * OUTER], fp32)
        wb = late[:, :].rearrange("p (k o) -> p k o", k=PAIR_TILES + 1)
        z_sb = late[:, 0:2 * CB].rearrange("p (m b) -> p m b", m=2)
        h1_sb = late[:, 2 * CB:6 * CB].rearrange("p (m b) -> p m b", m=4)
        h2_sb = late[:, 6 * CB:8 * CB].rearrange("p (m b) -> p m b", m=2)
        w_sum = sb("w_sum", [P, OUTER], fp32)
        w_last = sb("w_last", [P, OUTER], fp32r)
        w1_sb = sb("w1_sb", [P, OUTER // P, HID1], fp32)
        w1d_raw = sb("w1d_raw", [DENSE, HID1], fp32)
        w1d_parts = sb("w1d_parts", [DENSE, 2, HID1], fp32r)
        w1d_four = sb("w1d_four", [4 * DENSE, HID1], fp32)
        w1d_sb = sb("w1d_sb", [4 * DENSE, HID1], fp32r)
        w2_sb = sb("w2_sb", [P, HID1 // P, HID2], fp32)
        w3_sb = sb("w3_sb", [P, HID2 // P], fp32)
        b1_sb = sb("b1_sb", [P, HID1 // P], fp32)
        b2_sb = sb("b2_sb", [P, HID2 // P], fp32)
        dense_raw = sb("dense_raw", [4 * DENSE, BATCH], fp32)
        dense_sb = sb("dense_sb", [4 * DENSE, BATCH], fp32r)
        acc_sb = sb("acc_sb", [P, CB], fp32)
        s_rep = sb("s_rep", [P, CB], fp32)
        s_parts = sb("s_parts", [P, CB], fp32r)
        prod = sb("prod", [P, PRODS, CB], fp32)
        prod_last = sb("prod_last", [P, CB], fp32r)
        y_sb = sb("y_sb", [1, BATCH], fp32)

        acc_ps = ps("acc_ps", [P, CHUNKS, CB])
        rot_ps = ps("rot_ps", [P, 2, CB])
        z_ps = ps("z_ps", [P, 2, CB])

        index_landed = [sem(f"index_landed{i}") for i in range(GATHER_SLOTS)]
        ids_landed = sem("ids_landed")
        ids_cast = sem("ids_cast")
        ids_stored = sem("ids_stored")
        ids_bc_landed = [sem(f"ids_bc_landed{i}") for i in range(2)]
        row_landed = sem("row_landed")
        const_landed = sem("const_landed")
        table_landed = [sem(f"table_landed{i}") for i in range(2)]
        pair_w_landed = sem("pair_w_landed")
        dense_landed = sem("dense_landed")
        weight_landed = sem("weight_landed")
        tile_landed = [sem(f"tile_landed{i}") for i in range(GATHER_SLOTS)]
        tiles_begun = sem("tiles_begun")
        slot_free = sem("slot_free")
        high_ready = sem("high_ready")
        low_ready = sem("low_ready")
        direct_ready = sem("direct_ready")
        narrow_ready = sem("narrow_ready")
        wide_ready = sem("wide_ready")
        hot_free = sem("hot_free")
        cold_added = sem("cold_added")
        acc_copied = sem("acc_copied")
        fold_done = sem("fold_done")
        rep_copied = sem("rep_copied")
        s_high_ready = sem("s_high_ready")
        s_parts_ready = sem("s_parts_ready")
        pair_w_ready = sem("pair_w_ready")
        w_last_ready = sem("w_last_ready")
        dense_high = sem("dense_high")
        w1d_ready = sem("w1d_ready")
        dense_ready = sem("dense_ready")
        w1d_placed = sem("w1d_placed")
        w1d_copied = sem("w1d_copied")
        turns_ready = sem("turns_ready")
        rot_done = sem("rot_done")
        prod_ready = sem("prod_ready")
        last_high = sem("last_high")
        prod_used = sem("prod_used")
        z_copied = sem("z_copied")
        h1_done = sem("h1_done")
        h1_ready = sem("h1_ready")
        h2_done = sem("h2_done")
        h2_ready = sem("h2_ready")
        y_done = sem("y_done")
        y_copied = sem("y_copied")
        out_landed = sem("out_landed")

        STEPS = PAIR_TILES + 1
        block = ctx.enter_context(nc.Block())

        def next_rows(g):
            return SEGMENTS[g + 1][2] if g + 1 < len(SEGMENTS) else None

        @block.sync
        def _(sp):
            ids_tiles = ids.rearrange("(t p) f -> p t f", p=P)

            def load_table(n):
                sp.dma_start(stage[0:ROWS_P, n % 2, 0:J[n] * EMB],
                             tables[hot[n]].rearrange("(p j) e -> p (j e)", j=J[n])).then_inc(table_landed[n % 2], 16)

            def load_ids(n):
                sp.dma_start(ids_bc[:, n % 2, :], bass.AP(ids_rows, n * BATCH, [[0, P], [1, BATCH]]))\
                    .then_inc(ids_bc_landed[n % 2], 16)

            def next_indices(begin, end):
                for t in range(begin, end):
                    sp.wait_ge(tile_landed[t % GATHER_SLOTS], t // GATHER_SLOTS * 16 * COLD)
                    sp.dma_start(index[:, t % GATHER_SLOTS, :], ids_tiles[:, t, :])\
                        .then_inc(index_landed[t % GATHER_SLOTS], 16)

            sp.dma_start(ids_raw[:, :], bass.AP(ids_hot.tensor, 0, [[FLAT, P], [1, FLAT]])).then_inc(ids_landed, 16)
            sp.dma_start(index[:, 0, :], ids_tiles[:, 0, :]).then_inc(index_landed[0], 16)
            load_table(0)
            sp.dma_start(row_sb[:, :], row_of).then_inc(row_landed, 16)
            load_table(1)
            sp.wait_ge(ids_cast, 1)
            sp.dma_start(bass.AP(ids_rows, 0, [[FLAT, P], [1, FLAT]]), ids_h[:, :]).then_inc(ids_stored, 16)
            sp.wait_ge(ids_stored, 16)
            load_ids(0)
            load_ids(1)
            for u in range(1, GATHER_SLOTS):
                sp.dma_start(index[:, u, :], ids_tiles[:, u, :]).then_inc(index_landed[u], 16)
            for n in range(2, N_HOT):
                sp.wait_ge(low_ready, n - 1)
                load_table(n)
                sp.wait_ge(narrow_ready, START[n - 1] // 2)
                load_ids(n)
                if n == 4:
                    sp.dma_start(eye_sb[:, :], eye).then_inc(const_landed, 16)
                    sp.dma_start(fold_sb[:, :], fold_of).then_inc(const_landed, 16)
                    sp.dma_start(turn_sb[:, :], turns).then_inc(const_landed, 16)
                    sp.dma_start(wa[:, :, :], pair_a).then_inc(pair_w_landed, 16)
                if n == 6:
                    sp.dma_start(wb[0:EMB, 0, :], pair_b[0:EMB, 0, :]).then_inc(pair_w_landed, 16)
                    sp.dma_start(wb[:, 1:, :], pair_b[:, 1:, :]).then_inc(pair_w_landed, 16)
                if n == 8:
                    for i in range(4):
                        sp.dma_start(dense_raw[i * DENSE:(i + 1) * DENSE, :], dense_t).then_inc(dense_landed, 16)
                    sp.dma_start(w1d_raw[:, :], w1[OUTER:OUTER + DENSE, :]).then_inc(dense_landed, 16)
                    sp.dma_start(w1_sb[:, :, :], w1[0:OUTER, :].rearrange("(k p) m -> p k m", p=P))\
                        .then_inc(weight_landed, 16)
                    sp.dma_start(w2_sb[:, :, :], w2.rearrange("(k p) m -> p k m", p=P)).then_inc(weight_landed, 16)
                    with nc.allow_non_contiguous_dma(reason="a few hundred single elements"):
                        sp.dma_start(w3_sb[:, :], w3.rearrange("(k p) o -> p (k o)", p=P)).then_inc(weight_landed, 16)
                        sp.dma_start(b1_sb[:, :], b1.rearrange("(k p) -> p k", p=P)).then_inc(weight_landed, 16)
                        sp.dma_start(b2_sb[:, :], b2.rearrange("(k p) -> p k", p=P)).then_inc(weight_landed, 16)

                if n == N_SMALL - 1:
                    next_indices(GATHER_SLOTS, GATHER_SLOTS + CHUNK_TILES)

            sp.wait_ge(w1d_ready, 2)
            for i in range(4):
                sp.dma_start(w1d_four[i * DENSE:(i + 1) * DENSE, :], w1d_parts[:, i % 2, :].bitcast(fp32))\
                    .then_inc(w1d_placed, 16)

            next_indices(GATHER_SLOTS + CHUNK_TILES, TILES)
            sp.wait_ge(y_copied, CHUNKS)
            sp.dma_start(out.rearrange("b o -> o b"), y_sb[:, :]).then_inc(out_landed, 16)
            sp.wait_ge(out_landed, 16)

        @block.gpsimd
        def _(pool):
            with pool.Fori(0, TILES // GATHER_SLOTS) as turn:
                for u in range(GATHER_SLOTS):
                    pool.wait_ge(index_landed[u], (turn + 1) * 16)
                    pool.wait_ge(slot_free, turn * GATHER_SLOTS + u + 1)
                    pool.sem_inc(tiles_begun, 1)
                    for g, f in enumerate(cold):
                        nc.gpsimd.indirect_dma_start(
                            out=gathered[:, u, g, :], out_offset=None, in_=tables[f],
                            in_offset=bass.IndirectOffsetOnAxis(ap=index[:, u, f:f + 1], axis=0),
                        ).then_inc(tile_landed[u], 16)

        def rows_of(h, j):
            return (stage[0:ROWS_P, h, 0:j * EMB].rearrange("p (j e) -> p j e", e=EMB),
                    halves[0:ROWS_P, h, 0:j, 0:EMB], halves[0:ROWS_P, h, 0:j, EMB:2 * EMB])

        @block.scalar
        def _(act):
            act.sem_inc(wide_ready, NARROW)

            def high(h, j):
                rows, hi, _ = rows_of(h, j)
                nc.scalar.activation(hi, rows, ACT.Copy).then_inc(high_ready, 1)

            def pair(g, m, behind):
                first, _, j_count = SEGMENTS[g]
                for h in range(2):
                    for j in range(j_count):
                        q = h * j_count + j
                        if j == j_count // 2 and (h == 0 or behind):
                            act.wait_ge(table_landed[1 - h], m * 16 + (first // 2 + 1 + h) * 16)
                            act.wait_ge(hot_free, m * (2 * j_count) + (BUILT[g] + h * j_count + SLOTS))
                            high(1 - h, behind if h else j_count)
                        if j % 2:
                            act.wait_ge(narrow_ready, m * j_count + (BUILT[g] // 2 + q // 2 + 1))
                            act.wait_ge(hot_free, m * (2 * j_count) + (BUILT[g] + q + 1))
                            nc.scalar.activation(onehot[0:ROWS_P, q % SLOTS, :], narrow[0:ROWS_P, q // 2 % NARROW, :],
                                                 ACT.Copy).then_inc(wide_ready, 1)

            act.wait_ge(table_landed[0], 16)
            high(0, J[0])
            for g, (_, n, j) in enumerate(SEGMENTS):
                with act.Fori(0, n // 2 - 1) as m:
                    pair(g, m, j)
                pair(g, n // 2 - 1, next_rows(g))

            act.wait_ge(weight_landed, 16 * 5)

            def relu(layer, sb_out, bank, bias, done, ready, count):
                act.wait_ge(done, count)
                nc.scalar.activation(sb_out, bank, ACT.Relu, bias=bias).then_inc(ready, 1)

            def hidden2(c, m):
                relu(2, h2_sb[:, m, :], z_ps[:, m, :], b2_sb[:, m:m + 1], h2_done, h2_ready, 2 * c + m + 1)

            def output(c):
                act.wait_ge(y_done, c + 1)
                nc.scalar.activation(y_sb[:, c * CB:(c + 1) * CB], acc_ps[0:1, c, :], ACT.Copy).then_inc(y_copied, 1)

            for c in range(CHUNKS):
                act.wait_ge(cold_added, c + 1)
                nc.scalar.activation(acc_sb[:, :], acc_ps[:, c, :], ACT.Copy).then_inc(acc_copied, 1)
                if c:
                    hidden2(c - 1, 0)
                act.wait_ge(fold_done, c + 1)
                nc.scalar.activation(s_rep[:, :], rot_ps[:, 1, :], ACT.Copy).then_inc(rep_copied, 1)
                if c:
                    hidden2(c - 1, 1)
                    output(c - 1)
                act.wait_ge(prod_used, (c + 1) * STEPS)
                for m in range(2):
                    nc.scalar.activation(z_sb[:, m, :], z_ps[:, m, :], ACT.Copy).then_inc(z_copied, 1)
                for m in range(4):
                    relu(1, h1_sb[:, m, :], (rot_ps, z_ps)[m // 2][:, m % 2, :], b1_sb[:, m:m + 1],
                         h1_done, h1_ready, 4 * c + m + 1)
            hidden2(CHUNKS - 1, 0)
            hidden2(CHUNKS - 1, 1)
            output(CHUNKS - 1)

        @block.vector
        def _(dve):
            dve.sem_inc(slot_free, GATHER_SLOTS)
            dve.wait_ge(ids_landed, 16)
            nc.vector.tensor_copy(ids_h[:, :], ids_raw[:, :]).then_inc(ids_cast, 1)
            dve.wait_ge(row_landed, 16)

            def low(h, j):
                rows, hi, lo = rows_of(h, j)
                nc.vector.tensor_tensor(lo, rows, hi.bitcast(fp32), ALU.subtract).then_inc(low_ready, 1)

            def pair(g, m, behind):
                first, _, j_count = SEGMENTS[g]
                for h in range(2):
                    dve.wait_ge(ids_bc_landed[h], m * 16 + (first // 2 + 1) * 16)
                    for j in range(j_count):
                        q = h * j_count + j
                        if j == j_count - 1 and (h == 0 or behind):
                            dve.wait_ge(high_ready, m * 2 + (first + h + 2))
                            low(1 - h, behind if h else j_count)
                        column = (j_count - SMALL_J) * SMALL_J // 2 + j
                        if j % 2:
                            dve.wait_ge(wide_ready, m * j_count + (BUILT[g] // 2 + q // 2 + 1))
                            target, ready = narrow[0:ROWS_P, q // 2 % NARROW, :], narrow_ready
                        else:
                            dve.wait_ge(hot_free, m * (2 * j_count) + (BUILT[g] + q + 1))
                            target, ready = onehot[0:ROWS_P, q % SLOTS, :], direct_ready
                        nc.vector.tensor_scalar(target, ids_bc[0:ROWS_P, h, :], row_sb[0:ROWS_P, column:column + 1],
                                                None, ALU.is_equal).then_inc(ready, 1)

            def sum_tile(t):
                slot = t % GATHER_SLOTS
                dve.wait_ge(tile_landed[slot], (t // GATHER_SLOTS + 1) * 16 * COLD)
                nc.vector.tensor_reduce(cold_sum[:, t, :], gathered[:, slot, :, :].rearrange("p g e -> p e g"),
                                        AX.X, ALU.add).then_inc(slot_free, 1)

            dve.wait_ge(high_ready, 1)
            low(0, J[0])
            for g, (_, n, j) in enumerate(SEGMENTS):
                with dve.Fori(0, n // 2 - 1) as m:
                    pair(g, m, j)
                pair(g, n // 2 - 1, next_rows(g))
                if g == 0:
                    for t in range(CHUNK_TILES):
                        sum_tile(t)
                if g == 1:
                    dve.wait_ge(dense_landed, 16 * 5)
                    nc.vector.tensor_copy(w1d_parts[:, 0, :], w1d_raw[:, :]).then_inc(w1d_ready, 1)
                    dve.wait_ge(w1d_ready, 1)
                    nc.vector.tensor_tensor(w1d_parts[:, 1, :], w1d_raw[:, :], w1d_parts[:, 0, :].bitcast(fp32),
                                            ALU.subtract).then_inc(w1d_ready, 1)

            def pair_weights(k):
                rows = P if k else EMB
                nc.vector.tensor_tensor(wa[0:rows, k, :], wa[0:rows, k, :], wb[0:rows, k, :], ALU.add)\
                    .then_inc(pair_w_ready, 1)

            def dense_parts(c):
                columns = slice(c * CB, (c + 1) * CB)
                nc.vector.tensor_copy(dense_sb[:, columns], dense_raw[:, columns]).then_inc(dense_high, 1)
                dve.wait_ge(dense_high, c + 1)
                low_half = dense_sb[2 * DENSE:4 * DENSE, columns]
                nc.vector.tensor_tensor(low_half, dense_raw[2 * DENSE:4 * DENSE, columns], low_half.bitcast(fp32),
                                        ALU.subtract).then_inc(dense_ready, 1)

            def last_weights():
                nc.vector.tensor_tensor(w_sum[:, :], wa[:, PAIR_TILES, :], wb[:, PAIR_TILES, :], ALU.add)\
                    .then_inc(w_last_ready, 1)
                dve.wait_ge(w_last_ready, 1)
                nc.vector.tensor_copy(w_last[:, :], w_sum[:, :]).then_inc(w_last_ready, 1)
                dve.wait_ge(w_last_ready, 2)
                for at in (ROTS, 3 * ROTS):
                    part = w_last[at:at + ROTS, :]
                    nc.vector.tensor_tensor(part, w_sum[at:at + ROTS, :], part.bitcast(fp32), ALU.subtract)\
                        .then_inc(w_last_ready, 1)

            BETWEEN = [PAIR_TILES // 4 + 3 * u for u in range(CHUNK_TILES)]

            def products(c):
                dve.wait_ge(rep_copied, c + 1)
                nc.vector.tensor_copy(s_parts[:, :], s_rep[:, :]).then_inc(s_high_ready, 1)
                dve.wait_ge(s_high_ready, c + 1)
                nc.vector.tensor_tensor(s_parts[EMB:P, :], s_rep[EMB:P, :], s_parts[EMB:P, :].bitcast(fp32),
                                        ALU.subtract).then_inc(s_parts_ready, 1)
                for k in range(STEPS):
                    n = c * STEPS + k
                    if c == 0 and k < PAIR_TILES:
                        pair_weights(k)
                    dve.wait_ge(rot_done, n + 1)
                    if n >= PRODS:
                        dve.wait_ge(prod_used, n + 1 - PRODS)
                    nc.vector.tensor_tensor(prod[:, n % PRODS, :], rot_ps[:, k % 2, :], s_rep[:, :], ALU.mult)\
                        .then_inc(prod_ready, 1)
                    if k == 1:
                        dense_parts(c)
                    if c == 0 and k == 2:
                        last_weights()
                    if c == 0 and k == BETWEEN[-1] + 1:
                        dve.wait_ge(w1d_placed, 16 * 4)
                        nc.vector.tensor_copy(w1d_sb[:, :], w1d_four[:, :]).then_inc(w1d_copied, 1)
                    if c == 0 and k in BETWEEN:
                        sum_tile(CHUNK_TILES + BETWEEN.index(k))
                last = prod[:, (c * STEPS + PAIR_TILES) % PRODS, :]
                dve.wait_ge(prod_ready, (c + 1) * STEPS)
                nc.vector.tensor_copy(prod_last[:, :], last).then_inc(last_high, 1)
                dve.wait_ge(last_high, 2 * c + 1)
                nc.vector.tensor_tensor(prod_last[EMB:P, :], last[EMB:P, :], prod_last[EMB:P, :].bitcast(fp32),
                                        ALU.subtract).then_inc(last_high, 1)

            dve.wait_ge(const_landed, 16 * 3)
            nc.vector.tensor_copy(turn_r[:, :], turn_sb[:, :]).then_inc(turns_ready, 1)
            dve.wait_ge(pair_w_landed, 16 * 3)
            for c in range(CHUNKS):
                products(c)
                if c and c + 1 < CHUNKS:
                    for u in range(CHUNK_TILES):
                        sum_tile((c + 1) * CHUNK_TILES + u)

        @block.tensor
        def _(pe):
            pe.sem_inc(hot_free, SLOTS)

            def pair(g, m):
                first, _, j_count = SEGMENTS[g]
                for h in range(2):
                    pe.wait_ge(low_ready, m * 2 + (first + h + 1))
                    for j in range(j_count):
                        q = h * j_count + j
                        if j % 2:
                            pe.wait_ge(wide_ready, m * j_count + (BUILT[g] // 2 + q // 2 + 1 + NARROW))
                        else:
                            pe.wait_ge(direct_ready, m * j_count + (BUILT[g] // 2 + q // 2 + 1))
                        for c in range(CHUNKS):
                            last = nc.tensor.matmul(acc_ps[:, c, :], halves[0:ROWS_P, h, j, :],
                                                    onehot[0:ROWS_P, q % SLOTS, c * CB:(c + 1) * CB],
                                                    start=isinstance(m, int) and g == 0 and q == 0, stop=False,
                                                    skip_group_check=True)
                        last.then_inc(hot_free, 1)

            for g, (_, n, _) in enumerate(SEGMENTS):
                if g == 0:
                    pair(0, 0)
                with pe.Fori(1 if g == 0 else 0, n // 2) as m:
                    pair(g, m)

            def add_cold(c):
                pe.wait_ge(slot_free, GATHER_SLOTS + (c + 1) * CHUNK_TILES)
                for u in range(CHUNK_TILES):
                    last = nc.tensor.matmul(acc_ps[0:EMB, c, u * P:(u + 1) * P], cold_sum[:, c * CHUNK_TILES + u, :],
                                            eye_sb[:, :], start=False, stop=u == CHUNK_TILES - 1, skip_group_check=True)
                last.then_inc(cold_added, 1)

            def fold(c):
                pe.wait_ge(acc_copied, c + 1)
                nc.tensor.matmul(rot_ps[:, 1, :], fold_sb[:, :], acc_sb[:, :], start=True, stop=True)\
                    .then_inc(fold_done, 1)

            def rotate(k):
                at = k if k < PAIR_TILES else SPAN
                nc.tensor.matmul(rot_ps[:, k % 2, :], turn_r[:, at:at + P], s_parts[:, :],
                                 start=True, stop=True).then_inc(rot_done, 1)

            def hidden1(c):
                for m in range(4):
                    bank = (rot_ps, z_ps)[m // 2][:, m % 2, :]
                    if m == 2:
                        pe.wait_ge(z_copied, 2 * c + 2)
                    nc.tensor.matmul(bank, w1d_sb[:, m * P:(m + 1) * P], dense_sb[:, c * CB:(c + 1) * CB],
                                     start=True, stop=False)
                    for k in range(2):
                        pe.wait_ge(z_copied, 2 * c + k + 1)
                        last = nc.tensor.matmul(bank, w1_sb[:, k, m * P:(m + 1) * P], z_sb[:, k, :],
                                                start=False, stop=k == 1)
                    last.then_inc(h1_done, 1)

            def hidden2(c, m):
                for k in range(4):
                    pe.wait_ge(h1_ready, 4 * c + max(k + 1, 3 + m))
                    last = nc.tensor.matmul(z_ps[:, m, :], w2_sb[:, k, m * P:(m + 1) * P], h1_sb[:, k, :],
                                            start=k == 0, stop=k == 3)
                last.then_inc(h2_done, 1)

            def output(c):
                for k in range(2):
                    pe.wait_ge(h2_ready, 2 * c + k + 1)
                    last = nc.tensor.matmul(acc_ps[0:1, c, :], w3_sb[:, k:k + 1], h2_sb[:, k, :],
                                            start=k == 0, stop=k == 1)
                last.then_inc(y_done, 1)

            pe.wait_ge(const_landed, 16 * 3)
            for c in range(CHUNKS):
                add_cold(c)
                if c:
                    hidden2(c - 1, 0)
                fold(c)
                if c:
                    hidden2(c - 1, 1)
                pe.wait_ge(s_parts_ready, c + 1)
                if c == 0:
                    pe.wait_ge(turns_ready, 1)
                rotate(0)
                rotate(1)
                if c:
                    output(c - 1)
                for k in range(STEPS):
                    n = c * STEPS + k
                    if c == 0 and k < PAIR_TILES:
                        pe.wait_ge(pair_w_ready, k + 1)
                    pe.wait_ge(prod_ready, n + 1)
                    if k == PAIR_TILES:
                        pe.wait_ge(last_high, 2 * c + 2)
                        if c == 0:
                            pe.wait_ge(w_last_ready, 4)
                    for m in range(2):
                        columns = slice(m * P, (m + 1) * P)
                        if k < PAIR_TILES:
                            last = nc.tensor.matmul(z_ps[:, m, :], wa[:, k, columns], prod[:, n % PRODS, :],
                                                    start=k == 0, stop=False)
                        else:
                            last = nc.tensor.matmul(z_ps[:, m, :], w_last[:, columns], prod_last[:, :],
                                                    start=False, stop=True)
                    last.then_inc(prod_used, 1)
                    if k + 2 < STEPS:
                        rotate(k + 2)
                if c == 0:
                    pe.wait_ge(weight_landed, 16 * 5)
                    pe.wait_ge(w1d_copied, 1)
                pe.wait_ge(dense_ready, c + 1)
                hidden1(c)
            hidden2(CHUNKS - 1, 0)
            hidden2(CHUNKS - 1, 1)
            output(CHUNKS - 1)


_FIELDS = 39
_TABLES = [f"tbl_{f}" for f in range(_FIELDS)]
_PLAIN = ["ids"] + _TABLES + ["W_top1", "b_top1", "W_top2", "b_top2", "W_top3"]


def pair_order():
    import numpy as np
    lane = np.arange(EMB)[:, None]
    k = np.arange(PAIR_TILES)[None, :]
    first_i, second_i = lane + 0 * k, (lane + TURN) % EMB + 0 * k
    i = np.concatenate([first_i, second_i])
    j = np.concatenate([first_i + TURN + k, second_i + k]) % EMB
    last = np.arange(ROTS)
    last_i = np.concatenate([last, last, (last + TURN) % ROTS, (last + TURN) % ROTS])[:, None]
    return np.concatenate([i, last_i], axis=1), np.concatenate([j, last_i + ROTS], axis=1)


def kernel(**inputs):
    import numpy as np
    import concourse.bacc as bacc
    from concourse.bass_utils import run_bass_kernel_spmd

    arrays = {f"in_{name}": np.ascontiguousarray(inputs[name]) for name in _PLAIN}
    hot, _ = split_tables([inputs[t].shape[0] for t in _TABLES])
    arrays["in_dense_t"] = np.ascontiguousarray(np.asarray(inputs["dense_ctx"]).T)
    arrays["in_ids_hot"] = np.ascontiguousarray(np.asarray(inputs["ids"]).T[hot])
    i, j = pair_order()
    pair_w = np.asarray(inputs["L0_rec_p_weight"])
    arrays["in_pair_a"] = np.ascontiguousarray(pair_w[i * EMB + j])
    arrays["in_pair_b"] = np.ascontiguousarray(pair_w[j * EMB + i])
    arrays["in_eye"] = np.eye(P, dtype=np.float32)
    half = np.arange(EMB)
    rep = np.concatenate([half, half + TURN])
    arrays["in_fold"] = (np.arange(P)[:, None] % EMB == rep[None, :] % EMB).astype(np.float32)
    takes = np.concatenate([np.arange(SPAN) + TURN, rep + ROTS])
    arrays["in_turns"] = (rep[:, None] % EMB == takes[None, :] % EMB).astype(np.float32)
    lane = np.arange(P)[:, None]
    arrays["in_row_of"] = np.concatenate(
        [lane * rows + np.arange(rows)[None, :] for rows in (SMALL_J, MID_J)], axis=1).astype(np.float32)

    nc = bacc.Bacc("TRN2", target_bir_lowering=False, num_devices=1)
    ap = {name: nc.dram_tensor(name, a.shape, mybir.dt.from_np(a.dtype), kind="ExternalInput").ap()
          for name, a in arrays.items()}
    y = nc.dram_tensor("y", (BATCH, 1), mybir.dt.float32, kind="ExternalOutput").ap()
    tower(nc, ap["in_dense_t"], ap["in_ids"], ap["in_ids_hot"], [ap[f"in_{t}"] for t in _TABLES], ap["in_W_top1"],
          ap["in_b_top1"], ap["in_W_top2"], ap["in_b_top2"], ap["in_W_top3"], ap["in_pair_a"], ap["in_pair_b"],
          ap["in_eye"], ap["in_fold"], ap["in_turns"], ap["in_row_of"], y)
    return run_bass_kernel_spmd(nc, [arrays], core_ids=[0]).results[0]["y"]
```

```python
import concourse.bass as bass
from concourse import mybir
from contextlib import ExitStack

BATCH = 2048
EMB = 64
OUTER = 256
HID1 = 512
HID2 = 256
DENSE = 16
P = 128

TILES = BATCH // P
CHUNK_TILES = 4
CHUNKS = TILES // CHUNK_TILES
CB = CHUNK_TILES * P
GATHER_SLOTS = 8
ROWS_P = 125

SMALL_J, MID_J = 8, 10
N_SMALL, N_MID = 16, 4
N_HOT = N_SMALL + N_MID
J = [SMALL_J] * N_SMALL + [MID_J] * N_MID
TWO = 2
START = [sum(J[:n]) // TWO for n in range(N_HOT)]
GROUPS = sum(J) // TWO
PASSES = 2
PASS_CHUNKS = CHUNKS // PASSES
WIDTH = PASS_CHUNKS * CB
SLOTS = SMALL_J // TWO
QUAD = 4
NARROW = SLOTS // 2

ROTS = EMB // 2
TURN = ROTS // 2
PAIR_TILES = ROTS // 2
PRODS = 3
SPAN = PAIR_TILES + P


def split_tables(rows):
    small = [f for f, r in enumerate(rows) if r == SMALL_J * ROWS_P][:N_SMALL]
    mid = [f for f, r in enumerate(rows) if r == MID_J * ROWS_P][:N_MID]
    hot = small + mid
    return hot, [f for f in range(len(rows)) if f not in hot]


def tower(nc, dense_t, ids, ids_hot, tables, w1, b1, w2, b2, w3, pair_a, pair_b, eye, fold_of, turns, row_of, out):
    fp32, bf16, fp16, i32 = mybir.dt.float32, mybir.dt.bfloat16, mybir.dt.float16, mybir.dt.int32
    fp32r = mybir.dt.float32r
    ALU = mybir.AluOpType
    ACT = mybir.ActivationFunctionType
    AX = mybir.AxisListType
    FIELDS = len(tables)
    hot, cold = split_tables([t.shape[0] for t in tables])
    COLD = len(cold)
    FLAT = N_HOT * BATCH // P

    ids_rows = nc.dram_tensor("ids_rows", (TWO, N_HOT, BATCH), fp16)

    with ExitStack() as ctx:
        def sb(name, shape, dt):
            return ctx.enter_context(nc.sbuf_tensor(name, shape, dt))

        def ps(name, shape):
            return ctx.enter_context(nc.psum_tensor(name, shape, fp32))

        def sem(name):
            return ctx.enter_context(nc.semaphore(name))

        index = sb("index", [P, GATHER_SLOTS, FIELDS], i32)
        gathered = sb("gathered", [P, GATHER_SLOTS, COLD, EMB], fp32)
        cold_sum = sb("cold_sum", [P, TILES, EMB], fp32)
        ids_raw = sb("ids_raw", [P, FLAT], i32)
        ids_h = sb("ids_h", [P, TWO, FLAT], fp16)
        ids_bc = sb("ids_bc", [P, 2, TWO * WIDTH], fp16)
        eye_sb = sb("eye_sb", [P, P], fp32)
        fold_sb = sb("fold_sb", [P, P], fp32)
        turn_sb = sb("turn_sb", [P, SPAN + P], fp32)
        turn_r = sb("turn_r", [P, SPAN + P], fp32r)
        row_sb = sb("row_sb", [P, SMALL_J + MID_J], fp32)
        stage = sb("stage", [P, 2, MID_J * EMB], fp32)
        halves = sb("halves", [P, QUAD, MID_J, 2 * EMB], fp32r)
        onehot = sb("onehot", [P, SLOTS, TWO * WIDTH], fp32r)
        narrow = sb("narrow", [P, NARROW, TWO * WIDTH], bf16)
        wa = sb("wa", [P, PAIR_TILES + 1, OUTER], fp32)
        late = sb("late", [P, (PAIR_TILES + 1) * OUTER], fp32)
        wb = late[:, :].rearrange("p (k o) -> p k o", k=PAIR_TILES + 1)
        ids_first = late[:, 0:WIDTH].bitcast(i32)
        z_sb = late[:, 0:2 * CB].rearrange("p (m b) -> p m b", m=2)
        h1_sb = late[:, 2 * CB:6 * CB].rearrange("p (m b) -> p m b", m=4)
        h2_sb = late[:, 6 * CB:8 * CB].rearrange("p (m b) -> p m b", m=2)
        w_sum = sb("w_sum", [P, OUTER], fp32)
        w_last = sb("w_last", [P, OUTER], fp32r)
        w1_sb = sb("w1_sb", [P, OUTER // P, HID1], fp32)
        w1d_parts = sb("w1d_parts", [DENSE, 2, HID1], fp32r)
        w1d_four = sb("w1d_four", [4 * DENSE, HID1], fp32)
        w1d_sb = sb("w1d_sb", [4 * DENSE, HID1], fp32r)
        w2_sb = sb("w2_sb", [P, HID1 // P, HID2], fp32)
        w3_sb = sb("w3_sb", [P, HID2 // P], fp32)
        b1_sb = sb("b1_sb", [P, HID1 // P], fp32)
        b2_sb = sb("b2_sb", [P, HID2 // P], fp32)
        dense_raw = sb("dense_raw", [4 * DENSE, BATCH], fp32)
        dense_sb = sb("dense_sb", [4 * DENSE, CB], fp32r)
        acc_sb = sb("acc_sb", [P, CB], fp32)
        w1d_raw = acc_sb[0:DENSE, 0:HID1]
        s_rep = sb("s_rep", [P, CB], fp32)
        s_parts = sb("s_parts", [P, CB], fp32r)
        prod = sb("prod", [P, PRODS, CB], fp32)
        prod_last = sb("prod_last", [P, CB], fp32r)
        y_sb = sb("y_sb", [1, BATCH], fp32)

        acc_ps = ps("acc_ps", [P, CHUNKS, CB])
        rot_ps = ps("rot_ps", [P, 2, CB])
        z_ps = ps("z_ps", [P, 2, CB])

        index_landed = [sem(f"index_landed{i}") for i in range(GATHER_SLOTS)]
        first_landed = sem("first_landed")
        ids_landed = sem("ids_landed")
        ids_cast = sem("ids_cast")
        ids_stored = sem("ids_stored")
        ids_bc_landed = [sem(f"ids_bc_landed{i}") for i in range(2)]
        row_landed = sem("row_landed")
        const_landed = sem("const_landed")
        table_landed = [sem(f"table_landed{i}") for i in range(2)]
        pair_w_landed = sem("pair_w_landed")
        dense_landed = sem("dense_landed")
        weight_landed = sem("weight_landed")
        tile_landed = [sem(f"tile_landed{i}") for i in range(GATHER_SLOTS)]
        tiles_begun = sem("tiles_begun")
        slot_free = sem("slot_free")
        high_ready = sem("high_ready")
        low_ready = sem("low_ready")
        direct_ready = sem("direct_ready")
        narrow_ready = sem("narrow_ready")
        wide_ready = sem("wide_ready")
        hot_free = sem("hot_free")
        cold_added = sem("cold_added")
        acc_copied = sem("acc_copied")
        fold_done = sem("fold_done")
        rep_copied = sem("rep_copied")
        s_high_ready = sem("s_high_ready")
        s_parts_ready = sem("s_parts_ready")
        pair_w_ready = sem("pair_w_ready")
        w_last_ready = sem("w_last_ready")
        dense_high = sem("dense_high")
        w1d_ready = sem("w1d_ready")
        dense_ready = sem("dense_ready")
        w1d_placed = sem("w1d_placed")
        w1d_copied = sem("w1d_copied")
        turns_ready = sem("turns_ready")
        rot_done = sem("rot_done")
        prod_ready = sem("prod_ready")
        last_high = sem("last_high")
        prod_used = sem("prod_used")
        z_copied = sem("z_copied")
        h1_done = sem("h1_done")
        h1_ready = sem("h1_ready")
        h2_done = sem("h2_done")
        h2_ready = sem("h2_ready")
        y_done = sem("y_done")
        y_copied = sem("y_copied")
        out_landed = sem("out_landed")

        STEPS = PAIR_TILES + 1
        PORTION = 2
        PORTIONS = PAIR_TILES // PORTION
        block = ctx.enter_context(nc.Block())

        VISITS = PASSES * N_HOT

        def groups_before(v):
            return v // N_HOT * GROUPS + START[v % N_HOT]

        def behind(v):
            return J[(v + 1) % N_HOT] if v + 1 < VISITS else None

        STRIDE = 2
        FIRST_MAIN = N_HOT + 2
        SECOND_MAIN = FIRST_MAIN + -(-STEPS // STRIDE) + 1

        @block.sync
        def _(sp):
            ids_tiles = ids.rearrange("(t p) f -> p t f", p=P)

            def load_table(v):
                n = v % N_HOT
                sp.dma_start(stage[0:ROWS_P, n % 2, 0:J[n] * EMB],
                             tables[hot[n]].rearrange("(p j) e -> p (j e)", j=J[n])).then_inc(table_landed[n % 2], 16)

            def load_ids(v):
                n = v % N_HOT
                sp.dma_start(ids_bc[:, n % 2, :].rearrange("p (a b) -> p a b", a=TWO),
                             bass.AP(ids_rows, n * BATCH + v // N_HOT * WIDTH,
                                     [[0, P], [N_HOT * BATCH, TWO], [1, WIDTH]]))\
                    .then_inc(ids_bc_landed[n % 2], 16)

            def next_indices(begin, end):
                for t in range(begin, end):
                    sp.wait_ge(tile_landed[t % GATHER_SLOTS], t // GATHER_SLOTS * 16 * COLD)
                    sp.dma_start(index[:, t % GATHER_SLOTS, :], ids_tiles[:, t, :])\
                        .then_inc(index_landed[t % GATHER_SLOTS], 16)

            sp.dma_start(index[:, 0, :], ids_tiles[:, 0, :]).then_inc(index_landed[0], 16)
            load_table(0)
            sp.dma_start(ids_first[:, :], bass.AP(ids_hot.tensor, 0, [[0, P], [1, WIDTH]])).then_inc(first_landed, 16)
            sp.dma_start(row_sb[:, :], row_of).then_inc(row_landed, 16)
            sp.dma_start(ids_raw[:, :], bass.AP(ids_hot.tensor, 0, [[FLAT, P], [1, FLAT]])).then_inc(ids_landed, 16)
            load_table(1)
            sp.wait_ge(ids_cast, 1)
            sp.dma_start(bass.AP(ids_rows, 0, [[FLAT, P], [N_HOT * BATCH, TWO], [1, FLAT]]), ids_h[:, :, :])\
                .then_inc(ids_stored, 16)
            sp.wait_ge(ids_stored, 16)
            load_ids(1)
            for u in range(1, GATHER_SLOTS):
                sp.dma_start(index[:, u, :], ids_tiles[:, u, :]).then_inc(index_landed[u], 16)
            for v in range(2, VISITS):
                sp.wait_ge(low_ready, v - 1)
                load_table(v)
                sp.wait_ge(direct_ready, (groups_before(v - 1) + 1) // 2)
                sp.wait_ge(narrow_ready, groups_before(v - 1) // 2)
                load_ids(v)
                if v == 4:
                    sp.dma_start(eye_sb[:, :], eye).then_inc(const_landed, 16)
                    sp.dma_start(fold_sb[:, :], fold_of).then_inc(const_landed, 16)
                    sp.dma_start(turn_sb[:, :], turns).then_inc(const_landed, 16)
                elif 5 <= v < 5 + PORTIONS:
                    tiles = slice((v - 5) * PORTION, (v - 4) * PORTION)
                    sp.dma_start(wa[:, tiles, :], pair_a[:, tiles, :]).then_inc(pair_w_landed, 16)
                    sp.dma_start(wb[:, tiles, :], pair_b[:, tiles, :]).then_inc(pair_w_landed, 16)
                elif v == 5 + PORTIONS:
                    sp.dma_start(wa[:, PAIR_TILES, :], pair_a[:, PAIR_TILES, :]).then_inc(pair_w_landed, 16)
                    sp.dma_start(wb[:, PAIR_TILES, :], pair_b[:, PAIR_TILES, :]).then_inc(pair_w_landed, 16)
                    for i in range(4):
                        sp.dma_start(dense_raw[i * DENSE:(i + 1) * DENSE, :], dense_t).then_inc(dense_landed, 16)
                    sp.dma_start(w1d_raw, w1[OUTER:OUTER + DENSE, :]).then_inc(dense_landed, 16)
                elif v == 6 + PORTIONS:
                    sp.dma_start(w1_sb[:, :, :], w1[0:OUTER, :].rearrange("(k p) m -> p k m", p=P))\
                        .then_inc(weight_landed, 16)
                elif v == 7 + PORTIONS:
                    sp.dma_start(w2_sb[:, :, :], w2.rearrange("(k p) m -> p k m", p=P)).then_inc(weight_landed, 16)
                    with nc.allow_non_contiguous_dma(reason="a few hundred single elements"):
                        sp.dma_start(w3_sb[:, :], w3.rearrange("(k p) o -> p (k o)", p=P)).then_inc(weight_landed, 16)
                        sp.dma_start(b1_sb[:, :], b1.rearrange("(k p) -> p k", p=P)).then_inc(weight_landed, 16)
                        sp.dma_start(b2_sb[:, :], b2.rearrange("(k p) -> p k", p=P)).then_inc(weight_landed, 16)
                if v == N_HOT:
                    next_indices(GATHER_SLOTS, GATHER_SLOTS + CHUNK_TILES)
                if v == FIRST_MAIN:
                    sp.wait_ge(w1d_ready, 2)
                    for i in range(4):
                        sp.dma_start(w1d_four[i * DENSE:(i + 1) * DENSE, :], w1d_parts[:, i % 2, :].bitcast(fp32))\
                            .then_inc(w1d_placed, 16)
                if v == SECOND_MAIN:
                    next_indices(GATHER_SLOTS + CHUNK_TILES, TILES)

            sp.wait_ge(y_copied, CHUNKS)
            sp.dma_start(out.rearrange("b o -> o b"), y_sb[:, :]).then_inc(out_landed, 16)
            sp.wait_ge(out_landed, 16)

        @block.gpsimd
        def _(pool):
            with pool.Fori(0, TILES // GATHER_SLOTS) as turn:
                for u in range(GATHER_SLOTS):
                    pool.wait_ge(index_landed[u], (turn + 1) * 16)
                    pool.wait_ge(slot_free, turn * GATHER_SLOTS + u + 1)
                    pool.sem_inc(tiles_begun, 1)
                    for g, f in enumerate(cold):
                        nc.gpsimd.indirect_dma_start(
                            out=gathered[:, u, g, :], out_offset=None, in_=tables[f],
                            in_offset=bass.IndirectOffsetOnAxis(ap=index[:, u, f:f + 1], axis=0),
                        ).then_inc(tile_landed[u], 16)

        def rows_of(v, j):
            return (stage[0:ROWS_P, v % 2, 0:j * EMB].rearrange("p (j e) -> p j e", e=EMB),
                    halves[0:ROWS_P, v % QUAD, 0:j, 0:EMB], halves[0:ROWS_P, v % QUAD, 0:j, EMB:2 * EMB])

        @block.scalar
        def _(act):
            act.sem_inc(wide_ready, NARROW)

            def high(v, j):
                rows, hi, _ = rows_of(v, j)
                nc.scalar.activation(hi, rows, ACT.Copy).then_inc(high_ready, 1)

            def widen(m, v, before, j_count, j_next, at_high):
                groups = j_count // TWO
                if j_next:
                    act.wait_ge(table_landed[(v + 1) % 2], m * (16 * QUAD // 2) + ((v + 1) // 2 + 1) * 16)
                    if at_high is not None:
                        act.wait_ge(hot_free, m * (QUAD * groups) + (at_high + SLOTS))
                    high(v + 1, j_next)
                for g in range(groups):
                    if (before + g) % 2:
                        act.wait_ge(narrow_ready, m * (2 * groups) + ((before + g) // 2 + 1))
                        act.wait_ge(hot_free, m * (QUAD * groups) + (before + g + 1))
                        nc.scalar.activation(onehot[0:ROWS_P, (before + g) % SLOTS, :],
                                             narrow[0:ROWS_P, (before + g) // 2 % NARROW, :], ACT.Copy)\
                            .then_inc(wide_ready, 1)

            def widen_visit(v):
                widen(0, v, groups_before(v), J[v % N_HOT], behind(v),
                      groups_before(v + 2 - QUAD) if v + 1 >= QUAD else None)

            act.wait_ge(table_landed[0], 16)
            high(0, J[0])
            for v in range(QUAD):
                widen_visit(v)
            with act.Fori(1, N_SMALL // QUAD - 1) as m:
                for v in range(QUAD):
                    widen(m, v, START[v], SMALL_J, SMALL_J, (v + 2 - QUAD) * (SMALL_J // TWO))
            for v in range(N_SMALL - QUAD, N_HOT):
                widen_visit(v)

            def relu(sb_out, bank, bias, done, ready, count):
                act.wait_ge(done, count)
                nc.scalar.activation(sb_out, bank, ACT.Relu, bias=bias).then_inc(ready, 1)

            def hidden2(c, m):
                relu(h2_sb[:, m, :], z_ps[:, m, :], b2_sb[:, m:m + 1], h2_done, h2_ready, 2 * c + m + 1)

            def output(c):
                act.wait_ge(y_done, c + 1)
                nc.scalar.activation(y_sb[:, c * CB:(c + 1) * CB], acc_ps[0:1, c, :], ACT.Copy).then_inc(y_copied, 1)

            def copy_sum(c):
                act.wait_ge(cold_added, c + 1)
                nc.scalar.activation(acc_sb[:, :], acc_ps[:, c, :], ACT.Copy).then_inc(acc_copied, 1)

            def copy_folded(c):
                act.wait_ge(fold_done, c + 1)
                nc.scalar.activation(s_rep[:, :], rot_ps[:, 1, :], ACT.Copy).then_inc(rep_copied, 1)

            def copy_outer(c):
                act.wait_ge(prod_used, (c + 1) * STEPS)
                for m in range(2):
                    nc.scalar.activation(z_sb[:, m, :], z_ps[:, m, :], ACT.Copy).then_inc(z_copied, 1)

            def hidden1(c):
                if c == 0:
                    act.wait_ge(weight_landed, 16 * 5)
                for m in range(4):
                    relu(h1_sb[:, m, :], (rot_ps, z_ps)[m // 2][:, m % 2, :], b1_sb[:, m:m + 1],
                         h1_done, h1_ready, 4 * c + m + 1)

            copy_sum(0)
            widen_visit(N_HOT)
            copy_folded(0)
            widen_visit(N_HOT + 1)
            for v in range(FIRST_MAIN, SECOND_MAIN):
                widen_visit(v)
            copy_outer(0)
            hidden1(0)
            widen_visit(SECOND_MAIN)
            copy_sum(1)
            hidden2(0, 0)
            copy_folded(1)
            hidden2(0, 1)
            output(0)
            for v in range(SECOND_MAIN + 1, VISITS):
                widen_visit(v)
            copy_outer(1)
            hidden1(1)
            for c in range(PASS_CHUNKS, CHUNKS):
                copy_sum(c)
                hidden2(c - 1, 0)
                copy_folded(c)
                hidden2(c - 1, 1)
                output(c - 1)
                copy_outer(c)
                hidden1(c)
            hidden2(CHUNKS - 1, 0)
            hidden2(CHUNKS - 1, 1)
            output(CHUNKS - 1)

        @block.vector
        def _(dve):
            dve.sem_inc(slot_free, GATHER_SLOTS)
            dve.wait_ge(first_landed, 16)
            nc.vector.tensor_copy(ids_bc[:, 0, 0:WIDTH], ids_first[:, :])
            nc.vector.tensor_scalar(ids_bc[:, 0, WIDTH:TWO * WIDTH], ids_first[:, :], 1.0, None, ALU.subtract)\
                .then_inc(ids_bc_landed[0], 16)
            dve.wait_ge(ids_landed, 16)
            nc.vector.tensor_copy(ids_h[:, 0, :], ids_raw[:, :])
            nc.vector.tensor_scalar(ids_h[:, 1, :], ids_raw[:, :], 1.0, None, ALU.subtract).then_inc(ids_cast, 1)
            dve.wait_ge(row_landed, 16)

            def low(v, j):
                rows, hi, lo = rows_of(v, j)
                nc.vector.tensor_tensor(lo, rows, hi.bitcast(fp32), ALU.subtract).then_inc(low_ready, 1)

            def build(m, v, before, j_count, j_next):
                groups = j_count // TWO
                dve.wait_ge(ids_bc_landed[v % 2], m * (16 * QUAD // 2) + (v // 2 + 1) * 16)
                for g in range(groups):
                    column = (j_count - SMALL_J) * SMALL_J // 2 + g * TWO
                    if (before + g) % 2:
                        dve.wait_ge(wide_ready, m * (2 * groups) + ((before + g) // 2 + 1))
                        target, ready = narrow[0:ROWS_P, (before + g) // 2 % NARROW, :], narrow_ready
                    else:
                        dve.wait_ge(hot_free, m * (QUAD * groups) + (before + g + 1))
                        target, ready = onehot[0:ROWS_P, (before + g) % SLOTS, :], direct_ready
                    nc.vector.tensor_scalar(target, ids_bc[0:ROWS_P, v % 2, :], row_sb[0:ROWS_P, column:column + 1],
                                            None, ALU.is_equal).then_inc(ready, 1)
                if j_next:
                    dve.wait_ge(high_ready, m * QUAD + (v + 2))
                    low(v + 1, j_next)

            def build_visit(v):
                build(0, v, groups_before(v), J[v % N_HOT], behind(v))

            def sum_tile(t):
                slot = t % GATHER_SLOTS
                dve.wait_ge(tile_landed[slot], (t // GATHER_SLOTS + 1) * 16 * COLD)
                nc.vector.tensor_reduce(cold_sum[:, t, :], gathered[:, slot, :, :].rearrange("p g e -> p e g"),
                                        AX.X, ALU.add).then_inc(slot_free, 1)

            def split_dense_weights():
                dve.wait_ge(dense_landed, 16 * 5)
                nc.vector.tensor_copy(w1d_parts[:, 0, :], w1d_raw).then_inc(w1d_ready, 1)
                dve.wait_ge(w1d_ready, 1)
                nc.vector.tensor_tensor(w1d_parts[:, 1, :], w1d_raw, w1d_parts[:, 0, :].bitcast(fp32),
                                        ALU.subtract).then_inc(w1d_ready, 1)

            dve.wait_ge(high_ready, 1)
            low(0, J[0])
            with dve.Fori(0, N_SMALL // QUAD - 1) as m:
                for v in range(QUAD):
                    build(m, v, START[v], SMALL_J, SMALL_J)
            for v in range(N_SMALL - QUAD, N_HOT):
                build_visit(v)
                if v == N_HOT - 3:
                    split_dense_weights()
                if v >= N_HOT - 2:
                    for u in range(2):
                        sum_tile((v - N_HOT) % 2 * 2 + u)

            def pair_weights(k):
                rows = P if k else EMB
                nc.vector.tensor_tensor(wa[0:rows, k, :], wa[0:rows, k, :], wb[0:rows, k, :], ALU.add)\
                    .then_inc(pair_w_ready, 1)

            def dense_parts(c):
                columns = slice(c * CB, (c + 1) * CB)
                nc.vector.tensor_copy(dense_sb[:, :], dense_raw[:, columns]).then_inc(dense_high, 1)
                dve.wait_ge(dense_high, c + 1)
                low_half = dense_sb[2 * DENSE:4 * DENSE, :]
                nc.vector.tensor_tensor(low_half, dense_raw[2 * DENSE:4 * DENSE, columns], low_half.bitcast(fp32),
                                        ALU.subtract).then_inc(dense_ready, 1)

            def last_weights():
                nc.vector.tensor_tensor(w_sum[:, :], wa[:, PAIR_TILES, :], wb[:, PAIR_TILES, :], ALU.add)\
                    .then_inc(w_last_ready, 1)
                dve.wait_ge(w_last_ready, 1)
                nc.vector.tensor_copy(w_last[:, :], w_sum[:, :]).then_inc(w_last_ready, 1)
                dve.wait_ge(w_last_ready, 2)
                for at in (ROTS, 3 * ROTS):
                    part = w_last[at:at + ROTS, :]
                    nc.vector.tensor_tensor(part, w_sum[at:at + ROTS, :], part.bitcast(fp32), ALU.subtract)\
                        .then_inc(w_last_ready, 1)

            def sum_parts(c):
                dve.wait_ge(rep_copied, c + 1)
                nc.vector.tensor_copy(s_parts[:, :], s_rep[:, :]).then_inc(s_high_ready, 1)
                dve.wait_ge(s_high_ready, c + 1)
                nc.vector.tensor_tensor(s_parts[EMB:P, :], s_rep[EMB:P, :], s_parts[EMB:P, :].bitcast(fp32),
                                        ALU.subtract).then_inc(s_parts_ready, 1)

            def product(c, k):
                n = c * STEPS + k
                if c == 0 and k < PAIR_TILES:
                    pair_weights(k)
                dve.wait_ge(rot_done, n + 1)
                if n >= PRODS:
                    dve.wait_ge(prod_used, n + 1 - PRODS)
                nc.vector.tensor_tensor(prod[:, n % PRODS, :], rot_ps[:, k % 2, :], s_rep[:, :], ALU.mult)\
                    .then_inc(prod_ready, 1)
                if k == 1:
                    dense_parts(c)
                if c == 0 and k == 3:
                    last_weights()
                if k == PAIR_TILES:
                    last = prod[:, n % PRODS, :]
                    dve.wait_ge(prod_ready, n + 1)
                    nc.vector.tensor_copy(prod_last[:, :], last).then_inc(last_high, 1)
                    dve.wait_ge(last_high, 2 * c + 1)
                    nc.vector.tensor_tensor(prod_last[EMB:P, :], last[EMB:P, :], prod_last[EMB:P, :].bitcast(fp32),
                                            ALU.subtract).then_inc(last_high, 1)

            def sums(c):
                for u in range(CHUNK_TILES):
                    sum_tile(c * CHUNK_TILES + u)

            build_visit(N_HOT)
            dve.wait_ge(const_landed, 16 * 3)
            nc.vector.tensor_copy(turn_r[:, :], turn_sb[:, :]).then_inc(turns_ready, 1)
            build_visit(N_HOT + 1)
            sum_parts(0)
            dve.wait_ge(pair_w_landed, 16 * 2 * (PORTIONS + 1))
            for v in range(FIRST_MAIN, SECOND_MAIN - 1):
                build_visit(v)
                for k in range((v - FIRST_MAIN) * STRIDE, min((v - FIRST_MAIN + 1) * STRIDE, STEPS)):
                    product(0, k)
            dve.wait_ge(w1d_placed, 16 * 4)
            nc.vector.tensor_copy(w1d_sb[:, :], w1d_four[:, :]).then_inc(w1d_copied, 1)
            build_visit(SECOND_MAIN - 1)
            sums(1)
            build_visit(SECOND_MAIN)
            sum_parts(1)
            for v in range(SECOND_MAIN, VISITS):
                if v > SECOND_MAIN:
                    build_visit(v)
                for k in range((v - SECOND_MAIN) * STRIDE, (v - SECOND_MAIN + 1) * STRIDE):
                    product(1, k)
            for k in range((VISITS - SECOND_MAIN) * STRIDE, STEPS):
                product(1, k)
            for c in range(PASS_CHUNKS, CHUNKS):
                sums(c)
                sum_parts(c)
                for k in range(STEPS):
                    product(c, k)

        @block.tensor
        def _(pe):
            pe.sem_inc(hot_free, SLOTS)

            def look_up(s, m, v, before, j_count, begin):
                groups = j_count // TWO
                pe.wait_ge(low_ready, m * QUAD + (v + 1))
                for g in range(groups):
                    count = m * (2 * groups) + ((before + g) // 2 + 1)
                    if (before + g) % 2:
                        pe.wait_ge(wide_ready, count + NARROW)
                    else:
                        pe.wait_ge(direct_ready, count)
                    for i in range(TWO):
                        for a in range(PASS_CHUNKS):
                            at = i * WIDTH + a * CB
                            last = nc.tensor.matmul(acc_ps[:, s * PASS_CHUNKS + a, :],
                                                    halves[0:ROWS_P, v % QUAD, g * TWO + i, :],
                                                    onehot[0:ROWS_P, (before + g) % SLOTS, at:at + CB],
                                                    start=begin and g == 0 and i == 0, stop=False,
                                                    skip_group_check=True)
                    last.then_inc(hot_free, 1)

            def look_up_visit(v):
                look_up(v // N_HOT, 0, v, groups_before(v), J[v % N_HOT], v % N_HOT == 0)

            for v in range(QUAD):
                look_up_visit(v)
            with pe.Fori(1, N_SMALL // QUAD) as m:
                for v in range(QUAD):
                    look_up(0, m, v, START[v], SMALL_J, False)
            for v in range(N_SMALL, N_HOT):
                look_up_visit(v)

            def add_cold(c):
                pe.wait_ge(slot_free, GATHER_SLOTS + (c + 1) * CHUNK_TILES)
                for u in range(CHUNK_TILES):
                    last = nc.tensor.matmul(acc_ps[0:EMB, c, u * P:(u + 1) * P], cold_sum[:, c * CHUNK_TILES + u, :],
                                            eye_sb[:, :], start=False, stop=u == CHUNK_TILES - 1, skip_group_check=True)
                last.then_inc(cold_added, 1)

            def fold(c):
                pe.wait_ge(acc_copied, c + 1)
                nc.tensor.matmul(rot_ps[:, 1, :], fold_sb[:, :], acc_sb[:, :], start=True, stop=True)\
                    .then_inc(fold_done, 1)

            def rotate(k):
                at = k if k < PAIR_TILES else SPAN
                nc.tensor.matmul(rot_ps[:, k % 2, :], turn_r[:, at:at + P], s_parts[:, :],
                                 start=True, stop=True).then_inc(rot_done, 1)

            def hidden1(c):
                pe.wait_ge(dense_ready, c + 1)

                def dense_term(m):
                    nc.tensor.matmul((rot_ps, z_ps)[m // 2][:, m % 2, :], w1d_sb[:, m * P:(m + 1) * P], dense_sb[:, :],
                                     start=True, stop=False)

                dense_term(0)
                dense_term(1)
                for m in range(4):
                    bank = (rot_ps, z_ps)[m // 2][:, m % 2, :]
                    if m >= 2:
                        dense_term(m)
                    for k in range(2):
                        pe.wait_ge(z_copied, 2 * c + k + 1)
                        last = nc.tensor.matmul(bank, w1_sb[:, k, m * P:(m + 1) * P], z_sb[:, k, :],
                                                start=False, stop=k == 1)
                    last.then_inc(h1_done, 1)

            def hidden2(c, m):
                for k in range(4):
                    pe.wait_ge(h1_ready, 4 * c + max(k + 1, 3 + m))
                    last = nc.tensor.matmul(z_ps[:, m, :], w2_sb[:, k, m * P:(m + 1) * P], h1_sb[:, k, :],
                                            start=k == 0, stop=k == 3)
                last.then_inc(h2_done, 1)

            def output(c):
                for k in range(2):
                    pe.wait_ge(h2_ready, 2 * c + k + 1)
                    last = nc.tensor.matmul(acc_ps[0:1, c, :], w3_sb[:, k:k + 1], h2_sb[:, k, :],
                                            start=k == 0, stop=k == 1)
                last.then_inc(y_done, 1)

            def rotate_first(c):
                pe.wait_ge(s_parts_ready, c + 1)
                if c == 0:
                    pe.wait_ge(turns_ready, 1)
                rotate(0)
                rotate(1)

            def outer_step(c, k):
                n = c * STEPS + k
                if c == 0 and k < PAIR_TILES:
                    pe.wait_ge(pair_w_ready, k + 1)
                pe.wait_ge(prod_ready, n + 1)
                if k == PAIR_TILES:
                    pe.wait_ge(last_high, 2 * c + 2)
                    if c == 0:
                        pe.wait_ge(w_last_ready, 4)
                for m in range(2):
                    columns = slice(m * P, (m + 1) * P)
                    if k < PAIR_TILES:
                        last = nc.tensor.matmul(z_ps[:, m, :], wa[:, k, columns], prod[:, n % PRODS, :],
                                                start=k == 0, stop=False)
                    else:
                        last = nc.tensor.matmul(z_ps[:, m, :], w_last[:, columns], prod_last[:, :],
                                                start=False, stop=True)
                last.then_inc(prod_used, 1)
                if k + 2 < STEPS:
                    rotate(k + 2)

            pe.wait_ge(const_landed, 16 * 3)
            add_cold(0)
            look_up_visit(N_HOT)
            fold(0)
            look_up_visit(N_HOT + 1)
            rotate_first(0)
            for v in range(FIRST_MAIN, SECOND_MAIN - 1):
                look_up_visit(v)
                for k in range((v - FIRST_MAIN) * STRIDE, min((v - FIRST_MAIN + 1) * STRIDE, STEPS)):
                    outer_step(0, k)
            look_up_visit(SECOND_MAIN - 1)
            pe.wait_ge(weight_landed, 16 * 5)
            pe.wait_ge(w1d_copied, 1)
            hidden1(0)
            add_cold(1)
            hidden2(0, 0)
            fold(1)
            hidden2(0, 1)
            rotate_first(1)
            output(0)
            for v in range(SECOND_MAIN, VISITS):
                look_up_visit(v)
                for k in range((v - SECOND_MAIN) * STRIDE, (v - SECOND_MAIN + 1) * STRIDE):
                    outer_step(1, k)
            for k in range((VISITS - SECOND_MAIN) * STRIDE, STEPS):
                outer_step(1, k)
            hidden1(1)
            for c in range(PASS_CHUNKS, CHUNKS):
                add_cold(c)
                hidden2(c - 1, 0)
                fold(c)
                hidden2(c - 1, 1)
                rotate_first(c)
                output(c - 1)
                for k in range(STEPS):
                    outer_step(c, k)
                hidden1(c)
            hidden2(CHUNKS - 1, 0)
            hidden2(CHUNKS - 1, 1)
            output(CHUNKS - 1)


_FIELDS = 39
_TABLES = [f"tbl_{f}" for f in range(_FIELDS)]
_PLAIN = ["ids"] + _TABLES + ["W_top1", "b_top1", "W_top2", "b_top2", "W_top3"]


def pair_order():
    import numpy as np
    lane = np.arange(EMB)[:, None]
    k = np.arange(PAIR_TILES)[None, :]
    first_i, second_i = lane + 0 * k, (lane + TURN) % EMB + 0 * k
    i = np.concatenate([first_i, second_i])
    j = np.concatenate([first_i + TURN + k, second_i + k]) % EMB
    last = np.arange(ROTS)
    last_i = np.concatenate([last, last, (last + TURN) % ROTS, (last + TURN) % ROTS])[:, None]
    return np.concatenate([i, last_i], axis=1), np.concatenate([j, last_i + ROTS], axis=1)


def kernel(**inputs):
    import numpy as np
    import concourse.bacc as bacc
    from concourse.bass_utils import run_bass_kernel_spmd

    arrays = {f"in_{name}": np.ascontiguousarray(inputs[name]) for name in _PLAIN}
    hot, _ = split_tables([inputs[t].shape[0] for t in _TABLES])
    arrays["in_dense_t"] = np.ascontiguousarray(np.asarray(inputs["dense_ctx"]).T)
    arrays["in_ids_hot"] = np.ascontiguousarray(np.asarray(inputs["ids"]).T[hot])
    i, j = pair_order()
    pair_w = np.asarray(inputs["L0_rec_p_weight"])
    arrays["in_pair_a"] = np.ascontiguousarray(pair_w[i * EMB + j])
    arrays["in_pair_b"] = np.ascontiguousarray(pair_w[j * EMB + i])
    arrays["in_eye"] = np.eye(P, dtype=np.float32)
    half = np.arange(EMB)
    rep = np.concatenate([half, half + TURN])
    arrays["in_fold"] = (np.arange(P)[:, None] % EMB == rep[None, :] % EMB).astype(np.float32)
    takes = np.concatenate([np.arange(SPAN) + TURN, rep + ROTS])
    arrays["in_turns"] = (rep[:, None] % EMB == takes[None, :] % EMB).astype(np.float32)
    lane = np.arange(P)[:, None]
    arrays["in_row_of"] = np.concatenate(
        [lane * rows + np.arange(rows)[None, :] for rows in (SMALL_J, MID_J)], axis=1).astype(np.float32)

    nc = bacc.Bacc("TRN2", target_bir_lowering=False, num_devices=1)
    ap = {name: nc.dram_tensor(name, a.shape, mybir.dt.from_np(a.dtype), kind="ExternalInput").ap()
          for name, a in arrays.items()}
    y = nc.dram_tensor("y", (BATCH, 1), mybir.dt.float32, kind="ExternalOutput").ap()
    tower(nc, ap["in_dense_t"], ap["in_ids"], ap["in_ids_hot"], [ap[f"in_{t}"] for t in _TABLES], ap["in_W_top1"],
          ap["in_b_top1"], ap["in_W_top2"], ap["in_b_top2"], ap["in_W_top3"], ap["in_pair_a"], ap["in_pair_b"],
          ap["in_eye"], ap["in_fold"], ap["in_turns"], ap["in_row_of"], y)
    return run_bass_kernel_spmd(nc, [arrays], core_ids=[0]).results[0]["y"]
```
